# Optimizing a Trainium2 kernel written in Bass

```python
import numpy as np
import jax
import jax.numpy as jnp

def _softmax(x, axis=-1):
    return jax.nn.softmax(x, axis=axis)

def _gelu(x):
    return jax.nn.gelu(x, approximate=True)

def _silu(x):
    return jax.nn.silu(x)

def _sigmoid(x):
    return jax.nn.sigmoid(x)

def _layernorm(x, axis=-1, eps=1e-05):
    m = jnp.mean(x, axis=axis, keepdims=True)
    v = jnp.var(x, axis=axis, keepdims=True)
    return (x - m) / jnp.sqrt(v + eps)

def _scatter_add(tgt, idx, src, axis=0):
    return tgt.at[idx].add(src)

def _segment_sum(src, seg, n):
    return jax.ops.segment_sum(src, seg, n)
kernel_name = 'mk_seq_preln_d1_jaxref_r8_5cc6df'

def setup_inputs(seed: int=0):
    np.random.seed(seed)
    _w = jnp.asarray

    def _L0_attn_setup():
        import jax, jax.numpy as jnp
        import numpy as np
        HEADS = 16
        DIM_HEAD = 64
        ROT_DIM = 32
        SCALE = DIM_HEAD ** (-0.5)

        def _rope(x):
            n = x.shape[2]
            inv_freq = 1.0 / 10000.0 ** (jnp.arange(0, ROT_DIM, 2, dtype=jnp.float32) / ROT_DIM)
            ang = jnp.arange(n, dtype=jnp.float32)[:, None] * inv_freq[None, :]
            cos, sin = (jnp.cos(ang), jnp.sin(ang))
            x_rot, x_pass = (x[..., :ROT_DIM], x[..., ROT_DIM:])
            x1 = x_rot[..., 0::2]
            x2 = x_rot[..., 1::2]
            y1 = x1 * cos - x2 * sin
            y2 = x2 * cos + x1 * sin
            y = jnp.stack([y1, y2], axis=-1).reshape(x_rot.shape)
            return jnp.concatenate([y, x_pass], axis=-1)
        key = jax.random.key(seed)
        ks = jax.random.split(key, 5)
        b, n, d = (4, 256, 128)
        inner = HEADS * DIM_HEAD
        return {'queries': jax.random.normal(ks[0], (b, n, d), jnp.float32), 'Wq': jax.random.normal(ks[1], (d, inner), jnp.float32) * d ** (-0.5), 'Wkv': jax.random.normal(ks[2], (d, 2 * inner), jnp.float32) * d ** (-0.5), 'Wout': jax.random.normal(ks[3], (inner, d), jnp.float32) * inner ** (-0.5), 'bout': jnp.zeros((d,), jnp.float32)}
    _L0_attn_in = _L0_attn_setup()

    def _L0_ffn_setup():
        import jax, jax.numpy as jnp
        import numpy as np
        D_MODEL, D_FF, RANK = (128, 512, 32)
        B, S = (4, 512)
        key = jax.random.key(seed)
        ks = jax.random.split(key, 7)
        return {'x': jax.random.normal(ks[0], (B, S, D_MODEL), dtype=jnp.float32), 'U1': jax.random.normal(ks[1], (D_MODEL, RANK), dtype=jnp.float32) * 0.02, 'V1': jax.random.normal(ks[2], (RANK, D_FF), dtype=jnp.float32) * 0.02, 'b1': jnp.zeros((D_FF,), dtype=jnp.float32), 'U2': jax.random.normal(ks[3], (D_FF, RANK), dtype=jnp.float32) * 0.02, 'V2': jax.random.normal(ks[4], (RANK, D_MODEL), dtype=jnp.float32) * 0.02, 'b2': jnp.zeros((D_MODEL,), dtype=jnp.float32)}
    _L0_ffn_in = _L0_ffn_setup()
    _d = {'L0_attn_queries': _L0_attn_in['queries'], 'L0_attn_Wq': _L0_attn_in['Wq'], 'L0_attn_Wkv': _L0_attn_in['Wkv'], 'L0_attn_Wout': _L0_attn_in['Wout'], 'L0_attn_bout': _L0_attn_in['bout'], 'L0_ffn_U1': _L0_ffn_in['U1'], 'L0_ffn_V1': _L0_ffn_in['V1'], 'L0_ffn_b1': _L0_ffn_in['b1'], 'L0_ffn_U2': _L0_ffn_in['U2'], 'L0_ffn_V2': _L0_ffn_in['V2'], 'L0_ffn_b2': _L0_ffn_in['b2']}
    _x0 = _d['L0_attn_queries']
    _d['L0_attn_queries'] = jax.random.normal(jax.random.fold_in(jax.random.key(seed), 1), (4, 1024, 128), dtype=_x0.dtype)
    del _x0
    return _d

def reference(L0_attn_queries, L0_attn_Wq, L0_attn_Wkv, L0_attn_Wout, L0_attn_bout, L0_ffn_U1, L0_ffn_V1, L0_ffn_b1, L0_ffn_U2, L0_ffn_V2, L0_ffn_b2):

    def _L0_attn_ref(queries, Wq, Wkv, Wout, bout):
        import jax, jax.numpy as jnp
        import numpy as np
        HEADS = 16
        DIM_HEAD = 64
        ROT_DIM = 32
        SCALE = DIM_HEAD ** (-0.5)

        def _rope(x):
            n = x.shape[2]
            inv_freq = 1.0 / 10000.0 ** (jnp.arange(0, ROT_DIM, 2, dtype=jnp.float32) / ROT_DIM)
            ang = jnp.arange(n, dtype=jnp.float32)[:, None] * inv_freq[None, :]
            cos, sin = (jnp.cos(ang), jnp.sin(ang))
            x_rot, x_pass = (x[..., :ROT_DIM], x[..., ROT_DIM:])
            x1 = x_rot[..., 0::2]
            x2 = x_rot[..., 1::2]
            y1 = x1 * cos - x2 * sin
            y2 = x2 * cos + x1 * sin
            y = jnp.stack([y1, y2], axis=-1).reshape(x_rot.shape)
            return jnp.concatenate([y, x_pass], axis=-1)
        b, n, _ = queries.shape
        q = queries @ Wq
        kv = queries @ Wkv
        k, v = jnp.split(kv, 2, axis=-1)
        split_heads = lambda t: t.reshape(b, n, HEADS, DIM_HEAD).transpose(0, 2, 1, 3)
        q, k, v = (split_heads(q), split_heads(k), split_heads(v))
        q, k = (_rope(q), _rope(k))
        sim = jnp.einsum('bhid,bhjd->bhij', q, k) * SCALE
        attn = jax.nn.softmax(sim, axis=-1)
        out = jnp.einsum('bhij,bhjd->bhid', attn, v)
        out = out.transpose(0, 2, 1, 3).reshape(b, n, HEADS * DIM_HEAD)
        return out @ Wout + bout

    def _L0_ffn_ref(x, U1, V1, b1, U2, V2, b2):
        import jax, jax.numpy as jnp
        import numpy as np
        D_MODEL, D_FF, RANK = (128, 512, 32)
        B, S = (4, 512)
        P = jnp.einsum('bsd,dr->bsr', x, U1)
        H = jax.nn.gelu(jnp.einsum('bsr,rf->bsf', P, V1) + b1)
        Q = jnp.einsum('bsf,fr->bsr', H, U2)
        return jnp.einsum('bsr,rd->bsd', Q, V2) + b2
    x = L0_attn_queries
    x = x + _L0_attn_ref(_layernorm(x, axis=-1), L0_attn_Wq, L0_attn_Wkv, L0_attn_Wout, L0_attn_bout)
    x = x + _L0_ffn_ref(_layernorm(x, axis=-1), L0_ffn_U1, L0_ffn_V1, L0_ffn_b1, L0_ffn_U2, L0_ffn_V2, L0_ffn_b2)
    return x

_drawn_inputs = setup_inputs


def setup_inputs(seed=0):
    import zlib

    import numpy as np

    out = dict(_drawn_inputs(seed))
    spreads = {'L0_attn_bout': (0.0, 0.1), 'L0_ffn_b1': (0.0, 0.8), 'L0_ffn_b2': (0.0, 0.336)}
    factors = {'L0_ffn_U1': 8.0, 'L0_ffn_V1': 8.0, 'L0_ffn_U2': 8.0, 'L0_ffn_V2': 8.0}
    for name, (base, spread) in spreads.items():
        noise = np.random.default_rng([zlib.crc32(name.encode()), seed]).standard_normal(out[name].shape)
        drawn = base * np.exp(spread * noise) if base else spread * noise
        out[name] = jnp.asarray(drawn.astype(out[name].dtype))
    for name, factor in factors.items():
        out[name] = (out[name] * factor).astype(out[name].dtype)
    return out
```

```python
from contextlib import ExitStack

import numpy as np

import concourse.bass as bass
from concourse import mybir
from concourse.alu_op_type import AluOpType as ALU

ACT = mybir.ActivationFunctionType
AX = mybir.AxisListType.X
F32, F16, BF16 = mybir.dt.float32, mybir.dt.float16, mybir.dt.bfloat16

B, N, D = 4, 1024, 128
HEADS, DH, ROT = 16, 64, 32
FF, RANK = 512, 32
P = 128
TILES = B * N // P
KT = N // P
GH = 4
GROUPS = B * HEADS // GH
GPB = HEADS // GH
QW = 256
SLOTS = GH * N // QW
VW = 2 * DH + 1
VP = VW + 1
WSCALE = 16.0
MSCALE = 4096.0
EXP_SCALE = DH ** -0.5 / (WSCALE * WSCALE)
EPS = 1e-5
UNITS = 16
HAND = 13 * 16
LEAD = 20

PROJ_AT = [(3, 3), (4, 0), (4, 1), (4, 3), (5, 0), (5, 1), (5, 3), (6, 0), (6, 1), (6, 3), (7, 0), (7, 3),
           (8, 0), (8, 1), (8, 3), (9, 0)]
PROJ = [(w, c, t) for w in "qk" for c in range(2) for t in ("rot", "swap", "pass")] + [("v", c, "v") for c in range(4)]
OUT_AT = {(4, 2): ("turn", 1, 0), (5, 2): ("turn", 1, 1), (6, 2): ("out", 1, 0), (7, 2): ("out", 1, 1),
          (12, 0): ("turn", 0, 0), (12, 2): ("turn", 0, 1), (13, 0): ("out", 0, 0), (13, 2): ("out", 0, 1)}
MAX_AT = [(3, 1), (7, 1), (11, 1), (15, 1)]
HAND_AT = {2: 3, 10: 0, 12: 1, 14: 2}


def tiles_of(first, last):
    out = []
    for k in range(SLOTS):
        for s in range(4):
            if (k, s) in PROJ_AT and not last:
                out.append((k, s, "proj", PROJ[PROJ_AT.index((k, s))]))
            if (k, s) in OUT_AT:
                kind, chunk, half = OUT_AT[k, s]
                if not (first and chunk == 1):
                    out.append((k, s, kind, (chunk, half)))
            if (k, s) in MAX_AT and not (last and k == SLOTS - 1):
                out += [(k, s, "max", (MAX_AT.index((k, s)), half)) for half in range(2)]
    return out


PRE_TILES = len(PROJ) + 2
FIRST_TILES = len(tiles_of(True, False))
MID_TILES = len(tiles_of(False, False))
assert PRE_TILES % 2 == 0 and FIRST_TILES % 2 == 0 and MID_TILES % 2 == 0


class Iteration:

    def __init__(self, i, first=False, last=False):
        self.i, self.first, self.last = i, first, last
        self.tiles = tiles_of(first, last)
        self.tile0 = PRE_TILES if first else PRE_TILES + FIRST_TILES + (i - 1) * MID_TILES

    def slot(self, k):
        return self.i * SLOTS + k

    def at(self, k, s):
        return [(n, t[2], t[3]) for n, t in enumerate(self.tiles) if t[:2] == (k, s)]

    def back(self, k, s, by):
        p = 4 * k + s - by
        return self.at(p // 4, p % 4) if p >= 0 else []


def build(nc, x_d, wq_d, wkv_d, wout_d, bout_d, u1_d, v1_d, b1_d, u2_d, v2_d, b2_d, rope_d, ident_d, out_d):
    with ExitStack() as ctx:
        def sb(name, shape, dt):
            return ctx.enter_context(nc.sbuf_tensor(name, shape, dt))

        def pb(name, shape, dt):
            return ctx.enter_context(nc.psum_tensor(name, shape, dt))

        def sem(name):
            return ctx.enter_context(nc.semaphore(name))

        X = sb("X", [P, TILES, D], F32)
        XT = sb("XT", [P, 2, B * N], F16)
        WQK = sb("WQK", [P, 2, 2, 3, HEADS * ROT], F16)
        WV = sb("WV", [P, 2, HEADS * DH], F16)
        WO = sb("WO", [P, HEADS * DH // P, D], F32)
        ROPE = sb("ROPE", [P, 2, N], F32)
        IDENT = sb("IDENT", [P, P], F32)
        IDENT16 = sb("IDENT16", [P, P], F16)
        BO = sb("BO", [P, D], F32)
        B2 = sb("B2", [P, D], F32)
        B1 = sb("B1", [P, FF // P], F32)
        B1R = sb("B1R", [FF // P, P], F32)
        U1 = sb("U1", [P, RANK], F32)
        V1 = sb("V1", [RANK, FF], F32)
        U2 = sb("U2", [P, FF // P, RANK], F32)
        V2 = sb("V2", [RANK, D], F32)
        WRAW = sb("WRAW", [P, 3, HEADS * DH], F32)
        KHH = sb("KHH", [P, GH, N], F16)
        QHL = sb("QHL", [P, GH, N], F16)
        KL1 = sb("KL1", [P, GH, N], F16)
        QHM = sb("QHM", [P, GH, N], F16)
        V = sb("V", [P, GH, KT * VP], F16)
        KS = sb("KS", [P, 2, 2, N], F16)
        QS = sb("QS", [P, 2, 2, N], F16)
        VS = sb("VS", [P, GH, KT * VP], F16)
        T1 = sb("T1", [P, 512], F32)
        T2 = sb("T2", [P, 512], F32)
        YR = sb("YR", [P, 512], F32)
        PF = sb("PF", [P, 4, 1024], F32)
        PR = sb("PR", [P, 4, 1024], F16)
        OS = sb("OS", [P, 2, 2, VW], F32)
        ON = sb("ON", [P, 2, DH], F32)
        RS = sb("RS", [P, 2], F32)
        OG = sb("OG", [P, 2, KT, P], F32)
        OT = sb("OT", [P, N], F32)
        MX = sb("MX", [P, 2, UNITS], F32)
        MJ = sb("MJ", [P, KT], F32)
        MN = sb("MN", [P, KT], F16)
        ST = sb("ST", [P, TILES, 6], F32)
        MV = sb("MV", [P, TILES, 2], F32)
        VE = sb("VE", [P, TILES], F32)
        MINUS_HALF = sb("MINUS_HALF", [P, TILES], F32)
        RSTD = sb("RSTD", [P, TILES], F32)
        XN = PF[:, :, :].rearrange("p a (t d) -> p (a t) d", d=D)
        XT2 = KHH[:, :, :].bitcast(F32).rearrange("p a b -> p (a b)")
        PT2 = QHL[:, :, :].bitcast(F32).rearrange("p a b -> p (a b)")
        HG = KS[:, :, :, :].bitcast(F32).rearrange("p a b c -> p (a b c)")
        HG2 = QS[:, :, :, :].bitcast(F32).rearrange("p a b c -> p (a b c)")
        QT2 = KL1[:, :, :].bitcast(F32).rearrange("p a b -> p (a b)")

        S = [pb(f"S{n}", [P, 2, QW], F32) for n in range(2)]
        M = [pb(f"M{n}", [P, 512], F32) for n in range(2)]
        O = [pb(f"O{n}", [P, 2, 256], F32) for n in range(2)]
        T = [pb(f"TILE{n}", [P, 512], F32) for n in range(2)]

        x_in = [sem(f"x_in{b}") for b in range(B)]
        w_in, wo_in, small_in, rope_in = sem("w_in"), sem("wo_in"), sem("small_in"), sem("rope_in")
        stats, aggr, var_eps, rstd, xn_made = (sem(n) for n in ("stats", "aggr", "var_eps", "rstd", "xn_made"))
        xt_made, xt_hi, xt_lo = sem("xt_made"), sem("xt_hi"), sem("xt_lo")
        w_hi, w_lo, w_swap, set_up, bias_in = sem("w_hi"), sem("w_lo"), sem("w_swap"), sem("set_up"), sem("bias_in")
        tile_made = sem("tile_made")
        rot_read, rot_sum, rot_hi, rot_lo = sem("rot_read"), sem("rot_sum"), sem("rot_hi"), sem("rot_lo")
        pass_hi, pass_lo, v_hi, v_lo = sem("pass_hi"), sem("pass_lo"), sem("v_hi"), sem("v_lo")
        turned, added, max_row = sem("turned"), sem("added"), sem("max_row")
        handed = [sem(f"handed{h}") for h in range(GH)]
        unit_made, unit_max, joined, max_scaled = sem("unit_made"), sem("unit_max"), sem("joined"), sem("max_scaled")
        scored, exped, rest_made = sem("scored"), sem("exped"), sem("rest_made")
        pv_done, o_copied, o_sum, o_recip, normed = sem("pv_done"), sem("o_copied"), sem("o_sum"), sem("o_recip"), sem("normed")
        f_stats, f_aggr, f_xn = sem("f_stats"), sem("f_aggr"), sem("f_xn")
        f_turn, f_xt, f_p, f_pc, f_h, f_g, f_q, f_qc, f_y, f_out = (
            sem(f"f_{n}") for n in ("turn", "xt", "p", "pc", "h", "g", "q", "qc", "y", "out"))
        f_bias, stored = sem("f_bias"), sem("stored")
        half_set = sem("half_set")
        b1_turned, b1_copied = sem("b1_turned"), sem("b1_copied")

        def wait(e, s, value):
            if not (isinstance(value, int) and value <= 0):
                e.wait_ge(s, value)

        def freed(kind, args, it):
            if kind == "proj":
                w, c, t = args
                g = it.i + 1
                if t in ("rot", "swap"):
                    return rot_read, g * 8 + ("qk".index(w) * 2 + c) * 2 + (t == "swap") + 1
                if t == "pass":
                    return pass_lo, g * 4 + "qk".index(w) * 2 + c + 1
                return v_lo, g * 4 + c + 1
            if kind == "max":
                return max_row, (it.i * GH + 1 + args[0]) * 2 + args[1] + 1
            chunk, half = args
            nth = (it.i * 2 - chunk) * 2 + half + 1
            return (turned if kind == "turn" else added), nth

        def before(it, n):
            if n >= 2:
                return it.tiles[n - 2][2:], it
            if it.first:
                return [("proj", PROJ[-2 + n]), ("max", (-1, n))][1], it
            return Iteration(it.i - 1).tiles[n - 2][2:], Iteration(it.i - 1)

        def proj_tile(e, args, g, bank):
            w, c, t = args
            gi, b = g % GPB, g // GPB
            if w == "v":
                for r in range(2):
                    rows = bass.ds(b * N + (2 * c + r) * P, P)
                    cols = bass.ds(gi * GH * DH, GH * DH)
                    for n, (xp, wp) in enumerate(((0, 0), (0, 1), (1, 0))):
                        mm = e.matmul(T[bank][:, r * 256:(r + 1) * 256], XT[:, xp, rows], WV[:, wp, cols],
                                      start=(n == 0), stop=(n == 2))
            else:
                rows, cols = bass.ds(b * N + c * 512, 512), bass.ds(gi * GH * ROT, GH * ROT)
                kind = ("rot", "swap", "pass").index(t)
                for n, (xp, wp) in enumerate(((0, 0), (0, 1), (1, 0))):
                    mm = e.matmul(T[bank][:, :], WQK[:, "qk".index(w), wp, kind, cols], XT[:, xp, rows],
                                  start=(n == 0), stop=(n == 2))
            mm.then_inc(tile_made, 1)

        def max_tile(e, head, half, bank):
            if half == 0:
                e.wait_ge(max_scaled, head + 1)
            for j in range(4):
                mm = e.matmul(T[bank][DH:DH + 1, j * P:(j + 1) * P], MN[:, half * 4 + j:half * 4 + j + 1],
                              IDENT16[:, :], start=True, stop=True)
            mm.then_inc(tile_made, 1)

        def turn_tile(e, chunk, half, bank):
            for j in range(4):
                mm = e.transpose(T[bank][:, j * P:(j + 1) * P], OG[:, chunk, half * 4 + j, :], IDENT[:, :])
            mm.then_inc(tile_made, 1)

        def out_tile(e, chunk, half, bank, pair):
            for j in range(4):
                q = half * 4 + j
                mm = e.matmul(T[bank][:, j * P:(j + 1) * P], OT[:, q * P:(q + 1) * P], WO[:, pair, :],
                              start=True, stop=True)
            mm.then_inc(tile_made, 1)

        def pe_tiles(e, it, k, s):
            for n, kind, args in it.at(k, s):
                (kind0, args0), it0 = before(it, n)
                e.wait_ge(*freed(kind0, args0, it0))
                bank = n % 2
                if kind == "proj":
                    proj_tile(e, args, it.i + 1, bank)
                elif kind == "max":
                    max_tile(e, it.i * GH + 1 + args[0], args[1], bank)
                elif kind == "turn":
                    chunk, half = args
                    e.wait_ge(normed, it.slot(8 if chunk == 0 else 0))
                    turn_tile(e, chunk, half, bank)
                else:
                    chunk, half = args
                    e.wait_ge(*freed("turn", (chunk, 1), it))
                    out_tile(e, chunk, half, bank, ((it.i - chunk) % GPB) * 2 + chunk)

        def pe_scores(e, it, k, s):
            n, h, quarter = it.slot(k), k // 4, k % 4
            if quarter == 0 and s == 0:
                e.wait_ge(max_row, (it.i * GH + h) * 2 + 2)
            wait(e, exped, 4 * n + s - 1)
            for kk in range(2):
                keys = slice((2 * s + kk) * P, (2 * s + kk + 1) * P)
                rows = slice(quarter * QW, (quarter + 1) * QW)
                e.matmul(S[s % 2][:, kk, :], KHH[:, h, keys], QHL[:, h, rows], start=True, stop=False)
                mm = e.matmul(S[s % 2][:, kk, :], KL1[0:DH + 1, h, keys], QHM[0:DH + 1, h, rows],
                              start=False, stop=True)
            mm.then_inc(scored, 1)

        def pe_values(e, n, k, s):
            qt, half, h, bank = s % 2, s // 2, (k % SLOTS) // 4, k % 2
            if s == 0:
                wait(e, o_copied, n - 1)
            if qt == 0:
                e.wait_ge(rest_made, 2 * n + half + 1)
            buf = (2 * k + half) % 4
            hi = PF[:, buf, :].bitcast(BF16)
            for j in range(4):
                kt = half * 4 + j
                at = j * QW + qt * P
                vals = V[:, h, kt * VP:kt * VP + VW]
                e.matmul(O[bank][:, qt, 0:VW], hi[:, 2 * at + 1:2 * (at + P):2], vals,
                         start=(s == 0 and j == 0), stop=False, skip_group_check=True)
                mm = e.matmul(O[bank][:, qt, 0:VW], PR[:, buf, at:at + P], vals,
                              start=False, stop=(half == 1 and j == 3), skip_group_check=True)
            if s == 3:
                mm.then_inc(pv_done, 1)

        def pe_slot(e, it, k):
            for s in range(4):
                if not it.first or k > 0:
                    pe_values(e, it.slot(k - 1), k - 1, s)
                pe_tiles(e, it, k, s)
                pe_scores(e, it, k, s)
                if not (it.last and 4 * k + LEAD + s >= GH * UNITS):
                    place_u = 4 * k + LEAD + s
                    fills = it.i + place_u // (GH * UNITS) + 1
                    u = it.slot(k) * 4 + LEAD + s
                    place, unit = (place_u // UNITS) % GH, place_u % UNITS
                    if unit == 0:
                        e.wait_ge(handed[place], HAND * fills)
                    e.wait_ge(unit_max, u - 1)
                    e.matmul(M[s % 2][:, :], QHL[:, place, (unit // 2) * P:(unit // 2 + 1) * P],
                             KHH[:, place, (unit % 2) * 512:(unit % 2 + 1) * 512],
                             start=True, stop=True).then_inc(unit_made, 1)

        def act_tile(e, kind, args, made, g, bank):
            if kind == "proj" and args[2] == "pass":
                w, c, _ = args
                st = (QS, KS)["qk".index(w)]
                e.wait_ge(tile_made, made)
                if w == "q" and c == 0:
                    wait(e, handed[GH - 1], HAND * g)
                e.activation(st[:, 0, 1, c * 512:(c + 1) * 512], T[bank][:, :], ACT.Copy).then_inc(pass_hi, 1)
            elif kind == "proj" and args[2] == "v":
                c = args[1]
                e.wait_ge(tile_made, made)
                for r in range(2):
                    dst = VS[:, :, :].rearrange("p h (t v) -> p h t v", v=VP)[:, :, 2 * c + r, 0:DH]
                    src = T[bank][:, r * 256:(r + 1) * 256].rearrange("p (h d) -> p h d", d=DH)
                    cp = e.activation(dst, src, ACT.Copy)
                cp.then_inc(v_hi, 1)

        def act_rot(e, args, g):
            w, c, _ = args
            st, nth = (QS, KS)["qk".index(w)], "qk".index(w) * 2 + c
            e.wait_ge(rot_sum, g * 4 + nth + 1)
            if nth == 0:
                wait(e, handed[GH - 1], HAND * g)
            e.activation(st[:, 0, 0, c * 512:(c + 1) * 512], YR[:, :], ACT.Copy).then_inc(rot_hi, 1)

        def act_max(e, head, place, half, made, bank):
            e.wait_ge(tile_made, made)
            e.activation(QHM[DH:DH + 1, place, half * 512:(half + 1) * 512], T[bank][DH:DH + 1, :],
                         ACT.Copy).then_inc(max_row, 1)

        def act_tiles(e, it, k, s):
            for n, kind, args in it.at(k, s):
                made, bank = it.tile0 + n + 1, n % 2
                if kind == "proj":
                    act_tile(e, kind, args, made, it.i + 1, bank)
                elif kind == "max":
                    if args[1] == 0:
                        wait(e, scored, (it.i * GH + 1 + args[0]) * 16 - 48)
                    act_max(e, None, (1 + args[0]) % GH, args[1], made, bank)
                elif kind == "turn":
                    e.wait_ge(tile_made, made)
                    e.activation(OT[:, args[1] * 512:(args[1] + 1) * 512], T[bank][:, :], ACT.Copy).then_inc(turned, 1)
            for n, kind, args in it.back(k, s, 2):
                if kind == "proj" and args[2] == "swap":
                    act_rot(e, args, it.i + 1)

        def act_copy_out(e, n, k):
            e.wait_ge(pv_done, n + 1)
            wait(e, normed, n - 1)
            e.activation(OS[:, k % 2, :, :], O[k % 2][:, :, 0:VW], ACT.Copy).then_inc(o_copied, 1)

        def act_slot(e, it, k):
            n = it.slot(k)
            for s in range(4):
                e.wait_ge(scored, 4 * n + s + 1)
                if s % 2 == 0:
                    wait(e, pv_done, n - 1)
                e.activation(PF[:, (2 * k + s // 2) % 4, (s % 2) * 512:(s % 2 + 1) * 512],
                             S[s % 2][:, :, :].rearrange("p a b -> p (a b)"), ACT.Exp,
                             scale=EXP_SCALE).then_inc(exped, 1)
                if s == 0 and (not it.first or k >= 2):
                    act_copy_out(e, it.slot(k - 2), k)
                act_tiles(e, it, k, s)

        def dve_tile(e, kind, args, made, g, bank):
            w, c, t = args
            nth = "qkv".index(w) * 2 + c
            cols = slice(c * 512, (c + 1) * 512)
            if t in ("rot", "swap"):
                e.wait_ge(tile_made, made)
                if t == "rot":
                    wait(e, rot_sum, g * 4 + nth)
                e.tensor_tensor((T1, T2)[t == "swap"][:, :], T[bank][:, :], ROPE[:, int(t == "swap"), cols],
                                ALU.mult).then_inc(rot_read, 1)
                if t == "swap":
                    e.wait_ge(rot_read, (g * 4 + nth) * 2 + 2)
                    wait(e, rot_lo, g * 4 + nth)
                    e.tensor_tensor(YR[:, :], T1[:, :], T2[:, :], ALU.add).then_inc(rot_sum, 1)
            elif t == "pass":
                st = (QS, KS)["qk".index(w)]
                e.wait_ge(pass_hi, g * 4 + nth + 1)
                e.tensor_tensor(st[:, 1, 1, cols], T[bank][:, :], st[:, 0, 1, cols], ALU.subtract).then_inc(pass_lo, 1)
            else:
                e.wait_ge(v_hi, g * 4 + c + 1)
                vs = VS[:, :, :].rearrange("p h (t v) -> p h t v", v=VP)
                for r in range(2):
                    src = T[bank][:, r * 256:(r + 1) * 256].rearrange("p (h d) -> p h d", d=DH)
                    tt = e.tensor_tensor(vs[:, :, 2 * c + r, DH:2 * DH], src, vs[:, :, 2 * c + r, 0:DH], ALU.subtract)
                tt.then_inc(v_lo, 1)

        def dve_rot(e, args, g):
            w, c, _ = args
            st, nth = (QS, KS)["qk".index(w)], "qk".index(w) * 2 + c
            cols = slice(c * 512, (c + 1) * 512)
            e.wait_ge(rot_hi, g * 4 + nth + 1)
            e.tensor_tensor(st[:, 1, 0, cols], YR[:, :], st[:, 0, 0, cols], ALU.subtract).then_inc(rot_lo, 1)

        def dve_tiles(e, it, k, s):
            for n, kind, args in it.back(k, s, 1):
                made, bank = it.tile0 + n + 1, n % 2
                if kind == "proj":
                    dve_tile(e, kind, args, made, it.i + 1, bank)
                elif kind == "out":
                    chunk, half = args
                    b = (it.i - chunk) // GPB
                    e.wait_ge(tile_made, made)
                    xs = X[:, bass.ds(b * KT + half * 4, 4), :]
                    e.tensor_tensor(xs, T[bank][:, :].rearrange("p (t d) -> p t d", d=D), xs, ALU.add).then_inc(added, 1)
            for n, kind, args in it.back(k, s, 3):
                if kind == "proj" and args[2] == "swap":
                    dve_rot(e, args, it.i + 1)

        def dve_unit(e, u, head, place_u):
            unit, side = place_u % UNITS, (place_u // UNITS) % 2
            e.wait_ge(unit_made, u + 1)
            e.tensor_reduce(MX[:, side, unit:unit + 1], M[unit % 2][:, :], AX, ALU.max).then_inc(unit_max, 1)
            if unit == UNITS - 1:
                e.wait_ge(unit_max, u + 1)
                e.tensor_reduce(MJ[:, :], MX[:, side, :].rearrange("p (q c) -> p q c", c=2), AX, ALU.max).then_inc(joined, 1)
                e.wait_ge(joined, head + 1)
                wait(e, max_row, 2 * head)
                e.tensor_scalar(MN[:, :], MJ[:, :], -1.0 / MSCALE, None, ALU.mult).then_inc(max_scaled, 1)

        def dve_rest(e, n, k, pair):
            buf = (2 * k + pair) % 4
            e.wait_ge(exped, 4 * n + 2 * pair + 2)
            e.tensor_tensor(PR[:, buf, :], PF[:, buf, :], PF[:, buf, :].bitcast(BF16)[:, 1:2048:2],
                            ALU.subtract).then_inc(rest_made, 1)

        def dve_norm(e, n, k):
            h, side = (k % SLOTS) // 4, k % 2
            e.wait_ge(o_copied, n + 1)
            wait(e, normed, n)
            e.tensor_tensor(ON[:, :, :], OS[:, side, :, 0:DH], OS[:, side, :, DH:2 * DH], ALU.add).then_inc(o_sum, 1)
            e.reciprocal(RS[:, :].rearrange("p (a b) -> p a b", b=1), OS[:, side, :, 2 * DH:VW]).then_inc(o_recip, 1)
            e.wait_ge(o_sum, n + 1)
            e.wait_ge(o_recip, n + 1)
            q = (k % 4) * 2
            for r in range(2):
                ts = e.tensor_scalar(OG[:, h // 2, q + r, (h % 2) * DH:(h % 2 + 1) * DH], ON[:, r, :],
                                     RS[:, r:r + 1], None, ALU.mult)
            ts.then_inc(normed, 1)

        def dve_slot(e, it, k):
            n = it.slot(k)
            for s in range(4):
                dve_tiles(e, it, k, s)
                place_u = 4 * k + s + LEAD - 1
                if not (it.last and place_u >= GH * UNITS):
                    dve_unit(e, 4 * n + s + LEAD - 1, it.i * GH + place_u // UNITS, place_u)
                if s == 0 and (not it.first or k > 0):
                    dve_rest(e, it.slot(k - 1), k - 1, 1)
                if s == 2:
                    dve_rest(e, n, k, 0)
                if s == 1 and (not it.first or k >= 2):
                    if (k - 2) % SLOTS == 0:
                        if not it.first:
                            e.wait_ge(*freed("turn", (0, 1), Iteration(it.i - 1)))
                    if k - 2 == 8 and not it.first:
                        e.wait_ge(*freed("turn", (1, 1), it))
                    dve_norm(e, it.slot(k - 2), k - 2)

        def hand_over(sp, h):
            rows = slice(32 * h, 32 * h + 32)
            for dst, st, top, hl in ((KHH, KS, 0, 0), (KHH, KS, DH, 0), (KL1, KS, 0, 1), (QHL, QS, 0, 0),
                                     (QHL, QS, DH, 1), (QHM, QS, 0, 0)):
                for t in range(2):
                    sp.dma_start(dst[top + 32 * t:top + 32 * t + 32, h, :], st[rows, hl, t, :]).then_inc(handed[h], 16)
            sp.dma_start(V[:, h, :], VS[:, h, :]).then_inc(handed[h], 16)

        def sp_iteration(sp, it):
            for k, h in HAND_AT.items():
                if (it.first if h == GH - 1 else it.last):
                    continue
                if h == 0:
                    sp.wait_ge(rot_lo, (it.i + 1) * 4 + 4)
                    sp.wait_ge(pass_lo, (it.i + 1) * 4 + 4)
                    sp.wait_ge(v_lo, (it.i + 1) * 4 + 4)
                sp.wait_ge(pv_done, (it.i - (h == GH - 1)) * 16 + 4 * h + 4)
                hand_over(sp, h)

        block = ctx.enter_context(nc.Block())

        def loop(e, body):
            body(e, Iteration(0, first=True))
            with e.Fori(1, GROUPS - 1) as i:
                body(e, Iteration(i))
            body(e, Iteration(GROUPS - 1, last=True))

        END = GROUPS * SLOTS
        end = Iteration(GROUPS)
        FC = B * N // 512
        tail0 = PRE_TILES + FIRST_TILES + (GROUPS - 2) * MID_TILES + len(tiles_of(False, True))
        assert tail0 % 2 == 0

        @block.sync
        def _(sp):
            xr = x_d.rearrange("b (t p) d -> p (b t) d", p=P)
            sp.dma_start(X[:, 0:KT, :], xr[:, 0:KT, :]).then_inc(x_in[0], 16)
            sp.dma_start(IDENT[:, :], ident_d).then_inc(rope_in, 16)
            sp.dma_start(WRAW[:, 1:3, :], wkv_d.rearrange("p (a n) -> p a n", a=2)).then_inc(w_in, 16)
            sp.dma_start(ROPE[:, :, :], rope_d.rearrange("p (a n) -> p a n", a=2)).then_inc(rope_in, 16)
            for b in range(1, B):
                sp.dma_start(X[:, b * KT:(b + 1) * KT, :], xr[:, b * KT:(b + 1) * KT, :]).then_inc(x_in[b], 16)
            sp.dma_start(WO[:, :, :], wout_d.rearrange("(c p) n -> p c n", p=P)).then_inc(wo_in, 16)
            sp.wait_ge(rot_lo, 4)
            sp.wait_ge(pass_lo, 4)
            sp.wait_ge(v_lo, 4)
            sp.wait_ge(set_up, 3)
            for h in range(GH):
                hand_over(sp, h)
            loop(sp, sp_iteration)
            for c in range(FC):
                sp.wait_ge(f_out, c + 1)
                sp.dma_start(out_d.rearrange("b (t p) d -> p (b t) d", p=P)[:, 4 * c:4 * c + 4, :],
                             X[:, 4 * c:4 * c + 4, :]).then_inc(stored, 16)
            sp.wait_ge(stored, 16 * FC)

        @block.gpsimd
        def _(pool):
            def take_rstd(nth, t0, t1):
                pool.wait_ge(var_eps, nth + 1)
                pool.tensor_tensor(RSTD[:, t0:t1], VE[:, t0:t1], MINUS_HALF[:, t0:t1], ALU.pow).then_inc(rstd, 1)

            pool.memset(MINUS_HALF[:, :], -0.5).then_inc(half_set, 1)
            pool.wait_ge(half_set, 1)
            take_rstd(0, 0, KT)
            pool.wait_ge(rstd, 1)
            pool.memset(KL1[DH:DH + 32, :, :], MSCALE).then_inc(set_up, 1)
            pool.wait_ge(set_up, 1)
            pool.memset(VS[:, :, :].rearrange("p h (t v) -> p h t v", v=VP)[:, :, :, 2 * DH:VP], WSCALE).then_inc(set_up, 1)
            pool.wait_ge(rope_in, 32)
            pool.tensor_copy(IDENT16[:, :], IDENT[:, :]).then_inc(set_up, 1)
            for w in range(2):
                pool.wait_ge(w_lo, 2 * w + 1)
                pair = WQK[:, w, :, 0, :].rearrange("p a (n e) -> p a n e", e=2)
                swap = WQK[:, w, :, 1, :].rearrange("p a (n e) -> p a n e", e=2)
                pool.tensor_scalar(swap[:, :, :, 0], pair[:, :, :, 1], -1.0, None, ALU.mult).then_inc(w_swap, 1)
                pool.tensor_copy(swap[:, :, :, 1], pair[:, :, :, 0]).then_inc(w_swap, 1)
            for b in range(1, B):
                take_rstd(b, b * KT, (b + 1) * KT)
            pool.wait_ge(small_in, 16 * 7)
            for b in range(B):
                pool.wait_ge(xn_made, b + 1)
                for t in range(KT):
                    xs = X[:, b * KT + t, :]
                    tt = pool.tensor_tensor(xs, xs, BO[:, :], ALU.add)
                tt.then_inc(bias_in, 1)
            take_rstd(B, 0, TILES)

        @block.scalar
        def _(act):
            act.dma_start(WRAW[:, 0, :], wq_d).then_inc(w_in, 16)
            act.dma_start(BO[:, :], bout_d.rearrange("(a n) -> a n", a=1).broadcast_to([P, D])).then_inc(small_in, 16)
            act.dma_start(B2[:, :], b2_d.rearrange("(a n) -> a n", a=1).broadcast_to([P, D])).then_inc(small_in, 16)
            act.dma_start(B1R[:, :], b1_d.rearrange("(c p) -> c p", p=P)).then_inc(small_in, 16)
            act.dma_start(U1[:, :], u1_d).then_inc(small_in, 16)
            act.dma_start(V1[:, :], v1_d).then_inc(small_in, 16)
            act.dma_start(U2[:, :, :], u2_d.rearrange("(c p) r -> p c r", p=P)).then_inc(small_in, 16)
            act.dma_start(V2[:, :], v2_d).then_inc(small_in, 16)

            def w_part(w):
                if w < 2:
                    src = WRAW[:, w, :].rearrange("p (h d) -> p h d", d=DH)
                    for kind, d0 in ((0, 0), (2, ROT)):
                        act.activation(WQK[:, w, 0, kind, :].rearrange("p (h d) -> p h d", d=ROT),
                                       src[:, :, d0:d0 + ROT], ACT.Copy, scale=WSCALE).then_inc(w_hi, 1)
                else:
                    act.activation(WV[:, 0, :], WRAW[:, 2, :], ACT.Copy, scale=WSCALE).then_inc(w_hi, 1)

            def xt_part(c):
                act.wait_ge(xt_made, c + 1)
                act.activation(XT[:, 0, c * 512:(c + 1) * 512], S[c % 2][:, :, :].rearrange("p a b -> p (a b)"),
                               ACT.Copy).then_inc(xt_hi, 1)

            act.wait_ge(w_in, 32)
            for w in range(3):
                w_part(w)
            xt_part(0)
            xt_part(1)
            for n, args in enumerate(PROJ):
                act_tile(act, "proj", args, n + 1, 0, n % 2)
                if args[2] == "pass":
                    act_rot(act, args, 0)
            for c in range(2, 8):
                xt_part(c)
            act.wait_ge(b1_turned, 1)
            act.activation(B1[:, :], M[0][:, 0:FF // P], ACT.Copy).then_inc(b1_copied, 1)
            act.wait_ge(handed[0], HAND)
            for half in range(2):
                act_max(act, 0, 0, half, len(PROJ) + half + 1, half)

            def body(e, it):
                for k in range(SLOTS):
                    act_slot(e, it, k)

            loop(act, body)
            act_copy_out(act, END - 2, SLOTS - 2)
            act_copy_out(act, END - 1, SLOTS - 1)
            for half in range(2):
                act.wait_ge(tile_made, tail0 + half + 1)
                act.activation(OT[:, half * 512:(half + 1) * 512], T[half][:, :], ACT.Copy).then_inc(turned, 1)
            for c in range(FC):
                act.wait_ge(f_turn, c + 1)
                act.activation(XT2[:, (c % 4) * 512:(c % 4 + 1) * 512], M[0][:, :], ACT.Copy).then_inc(f_xt, 1)
                for f in range(4):
                    act.wait_ge(f_h, 4 * c + f + 1)
                    if f == 0:
                        wait(act, f_q, c - 1)
                    act.activation((HG, HG2)[c % 2][:, f * 512:(f + 1) * 512],
                                   S[f % 2][:, :, :].rearrange("p a b -> p (a b)"), ACT.Gelu_apprx_tanh,
                                   bias=B1[:, f:f + 1]).then_inc(f_g, 1)

        @block.tensor
        def _(pe):
            def turn_x(c):
                pe.wait_ge(xn_made, c // 2 + 1)
                if c == 0:
                    pe.wait_ge(rope_in, 32)
                wait(pe, xt_lo, c - 1)
                for j in range(4):
                    mm = pe.transpose(S[c % 2][:, :, :].rearrange("p a b -> p (a b)")[:, j * P:(j + 1) * P],
                                      XN[:, c * 4 + j, :], IDENT[:, :])
                mm.then_inc(xt_made, 1)

            turn_x(0)
            turn_x(1)
            pe.wait_ge(xt_lo, 2)
            pe.wait_ge(w_swap, 4)
            pe.wait_ge(w_lo, 5)
            pre = Iteration(-1)
            for n, args in enumerate(PROJ):
                if n >= 2:
                    pe.wait_ge(*freed("proj", PROJ[n - 2], pre))
                proj_tile(pe, args, 0, n % 2)
            for c in range(2, 8):
                turn_x(c)
            pe.wait_ge(small_in, 16 * 7)
            pe.transpose(M[0][:, 0:FF // P], B1R[:, :], IDENT[0:FF // P, 0:FF // P]).then_inc(b1_turned, 1)
            pe.wait_ge(b1_copied, 1)
            pe.wait_ge(set_up, 3)
            for u in range(LEAD):
                if u % UNITS == 0:
                    pe.wait_ge(handed[u // UNITS], HAND)
                wait(pe, unit_max, u - 1)
                unit = u % UNITS
                pe.matmul(M[u % 2][:, :], QHL[:, u // UNITS, (unit // 2) * P:(unit // 2 + 1) * P],
                          KHH[:, u // UNITS, (unit % 2) * 512:(unit % 2 + 1) * 512],
                          start=True, stop=True).then_inc(unit_made, 1)
                if u == UNITS + 1:
                    for half in range(2):
                        pe.wait_ge(*freed("proj", PROJ[len(PROJ) - 2 + half], pre))
                        max_tile(pe, 0, half, half)
            pe.wait_ge(xt_lo, 8)

            def body(e, it):
                for k in range(SLOTS):
                    if k == 4 and it.first:
                        e.wait_ge(wo_in, 16)
                    pe_slot(e, it, k)

            loop(pe, body)
            for s in range(4):
                pe_values(pe, END - 1, SLOTS - 1, s)
            pe.wait_ge(normed, END)
            lastit = Iteration(GROUPS - 1, last=True)
            for half in range(2):
                kind, args = lastit.tiles[half - 2][2:]
                pe.wait_ge(*freed(kind, args, lastit))
                turn_tile(pe, 1, half, half)
            pe.wait_ge(turned, GROUPS * 4)
            for half in range(2):
                out_tile(pe, 1, half, half, HEADS // 2 - 1)
            pe.wait_ge(unit_max, 64 * UNITS)
            pe.wait_ge(exped, 4 * END)

            def part_a(c):
                pe.wait_ge(f_xn, c + 1)
                wait(pe, f_xt, c)
                for j in range(4):
                    mm = pe.transpose(M[0][:, j * P:(j + 1) * P], XN[:, (4 * c + j) % 32, :], IDENT[:, :])
                mm.then_inc(f_turn, 1)
                pe.wait_ge(f_xt, c + 1)
                wait(pe, f_pc, c)
                pe.matmul(M[1][0:RANK, :], U1[:, :], XT2[:, (c % 4) * 512:(c % 4 + 1) * 512],
                          start=True, stop=True).then_inc(f_p, 1)

            def part_b(c):
                pe.wait_ge(f_pc, c + 1)
                for f in range(4):
                    wait(pe, f_g, 4 * c + f - 1)
                    pe.matmul(S[f % 2][:, :, :].rearrange("p a b -> p (a b)"), V1[:, f * P:(f + 1) * P],
                              PT2[0:RANK, (c % 4) * 512:(c % 4 + 1) * 512], start=True, stop=True).then_inc(f_h, 1)

            def part_c(c):
                wait(pe, f_qc, c)
                for f in range(4):
                    pe.wait_ge(f_g, 4 * c + f + 1)
                    mm = pe.matmul(O[0][0:RANK, :, :].rearrange("p a b -> p (a b)"), U2[:, f, :],
                                   (HG, HG2)[c % 2][:, f * 512:(f + 1) * 512], start=(f == 0), stop=(f == 3))
                mm.then_inc(f_q, 1)
                pe.wait_ge(f_qc, c + 1)
                wait(pe, f_out, c - 1) if c >= 2 else pe.wait_ge(added, GROUPS * 4)
                for j in range(4):
                    mm = pe.matmul(T[c % 2][:, j * P:(j + 1) * P],
                                   QT2[0:RANK, (c % 4) * 512 + j * P:(c % 4) * 512 + (j + 1) * P], V2[:, :],
                                   start=True, stop=True)
                mm.then_inc(f_y, 1)

            pe.wait_ge(o_copied, END)
            part_a(0)
            for c in range(FC):
                part_b(c)
                if c + 1 < FC:
                    part_a(c + 1)
                part_c(c)

        @block.vector
        def _(dve):
            def ln_stats(t0, t1, s1, s2, base):
                for t in range(t0, t1):
                    bs = dve.bn_stats(ST[:, t, :], X[:, t, :])
                bs.then_inc(s1, 1)
                dve.wait_ge(s1, base + 1)
                for t in range(t0, t1):
                    ba = dve.bn_aggr(MV[:, t, :], ST[:, t, :])
                ba.then_inc(s2, 1)
                dve.wait_ge(s2, base + 1)
                dve.tensor_scalar(VE[:, t0:t1], MV[:, t0:t1, 1], EPS, None, ALU.add).then_inc(var_eps, 1)

            def ln_apply(t0, t1, s):
                for t in range(t0, t1):
                    ts = dve.tensor_scalar(XN[:, t, :], X[:, t, :], MV[:, t, 0:1], RSTD[:, t:t + 1],
                                           ALU.subtract, ALU.mult)
                ts.then_inc(s, 1)

            def batch_stats(b):
                dve.wait_ge(x_in[b], 16)
                ln_stats(b * KT, (b + 1) * KT, stats, aggr, b)

            def batch_apply(b):
                dve.wait_ge(rstd, b + 1)
                ln_apply(b * KT, (b + 1) * KT, xn_made)

            def xt_part(c):
                dve.wait_ge(xt_hi, c + 1)
                cols = slice(c * 512, (c + 1) * 512)
                dve.tensor_tensor(XT[:, 1, cols], S[c % 2][:, :, :].rearrange("p a b -> p (a b)"), XT[:, 0, cols],
                                  ALU.subtract).then_inc(xt_lo, 1)

            batch_stats(0)
            batch_apply(0)
            dve.wait_ge(w_in, 32)
            for w in range(2):
                src = WRAW[:, w, :].rearrange("p (h d) -> p h d", d=DH)
                for n, (kind, d0) in enumerate(((0, 0), (2, ROT))):
                    dve.wait_ge(w_hi, 2 * w + n + 1)
                    hi, lo = (WQK[:, w, hl, kind, :].rearrange("p (h d) -> p h d", d=ROT) for hl in range(2))
                    dve.scalar_tensor_tensor(lo, src[:, :, d0:d0 + ROT], WSCALE, hi, ALU.mult,
                                             ALU.subtract).then_inc(w_lo, 1)
            xt_part(0)
            xt_part(1)
            dve.wait_ge(w_hi, 5)
            dve.scalar_tensor_tensor(WV[:, 1, :], WRAW[:, 2, :], WSCALE, WV[:, 0, :], ALU.mult,
                                     ALU.subtract).then_inc(w_lo, 1)
            for n, args in enumerate(PROJ):
                dve_tile(dve, "proj", args, n + 1, 0, n % 2)
                if args[2] == "pass":
                    dve_rot(dve, args, 0)
            for b in range(1, B):
                batch_stats(b)
            for b in range(1, B):
                batch_apply(b)
                xt_part(2 * b)
                xt_part(2 * b + 1)
            for u in range(LEAD - 1):
                dve_unit(dve, u, u // UNITS, u)

            def body(e, it):
                for k in range(SLOTS):
                    if it.first and k == 12:
                        e.wait_ge(bias_in, B)
                    dve_slot(e, it, k)

            loop(dve, body)
            dve_rest(dve, END - 1, SLOTS - 1, 1)
            dve_norm(dve, END - 2, SLOTS - 2)
            dve_norm(dve, END - 1, SLOTS - 1)
            for half in range(2):
                dve.wait_ge(tile_made, tail0 + 2 + half + 1)
                xs = X[:, (B - 1) * KT + half * 4:(B - 1) * KT + half * 4 + 4, :]
                dve.tensor_tensor(xs, T[half][:, :].rearrange("p (t d) -> p t d", d=D), xs, ALU.add).then_inc(added, 1)
            dve.wait_ge(added, GROUPS * 4)
            dve.wait_ge(pv_done, END)
            ln_stats(0, TILES, f_stats, f_aggr, 0)
            dve.wait_ge(rstd, B + 1)
            for c in range(FC):
                ln_apply(4 * c, 4 * c + 4, f_xn)
            dve.wait_ge(f_xn, FC)
            for t in range(TILES):
                tt = dve.tensor_tensor(X[:, t, :], X[:, t, :], B2[:, :], ALU.add)
            tt.then_inc(f_bias, 1)
            dve.wait_ge(f_bias, 1)

            def copy_p(c):
                dve.wait_ge(f_p, c + 1)
                dve.tensor_copy(PT2[0:RANK, (c % 4) * 512:(c % 4 + 1) * 512], M[1][0:RANK, :]).then_inc(f_pc, 1)

            copy_p(0)
            for c in range(FC):
                if c + 1 < FC:
                    copy_p(c + 1)
                dve.wait_ge(f_q, c + 1)
                dve.tensor_copy(QT2[0:RANK, (c % 4) * 512:(c % 4 + 1) * 512],
                                O[0][0:RANK, :, :].rearrange("p a b -> p (a b)")).then_inc(f_qc, 1)
                dve.wait_ge(f_y, c + 1)
                xs = X[:, 4 * c:4 * c + 4, :]
                dve.tensor_tensor(xs, T[c % 2][:, :].rearrange("p (t d) -> p t d", d=D), xs, ALU.add).then_inc(f_out, 1)


def rope_table():
    inv = np.float32(1.0) / np.float32(10000.0) ** (np.arange(0, ROT, 2, dtype=np.float32) / np.float32(ROT))
    ang = np.arange(N, dtype=np.float32)[:, None] * inv[None, :]
    both = [np.tile(np.repeat(f(ang).T, 2, axis=0), (GH, 1)) for f in (np.cos, np.sin)]
    return np.ascontiguousarray(np.concatenate(both, axis=1).astype(np.float32))


ROPE_TABLE = rope_table()
IDENTITY = np.eye(P, dtype=np.float32)

_INS = ["L0_attn_queries", "L0_attn_Wq", "L0_attn_Wkv", "L0_attn_Wout", "L0_attn_bout", "L0_ffn_U1", "L0_ffn_V1",
        "L0_ffn_b1", "L0_ffn_U2", "L0_ffn_V2", "L0_ffn_b2"]


def kernel(**inputs):
    import concourse.bacc as bacc
    from concourse.bass_utils import run_bass_kernel_spmd

    nc = bacc.Bacc("TRN2", target_bir_lowering=False, num_devices=1)
    arrays = {f"in_{n}": np.ascontiguousarray(inputs[n]) for n in _INS}
    arrays["in_rope"], arrays["in_ident"] = ROPE_TABLE, IDENTITY
    args = [nc.dram_tensor(n, a.shape, mybir.dt.from_np(a.dtype), kind="ExternalInput").ap() for n, a in arrays.items()]
    args.append(nc.dram_tensor("out", (B, N, D), F32, kind="ExternalOutput").ap())
    build(nc, *args)
    r = run_bass_kernel_spmd(nc, [arrays], core_ids=[0])
    return r.results[0]["out"]
```

```python
from contextlib import ExitStack

import numpy as np

import concourse.bass as bass
from concourse import mybir
from concourse.alu_op_type import AluOpType as ALU

ACT = mybir.ActivationFunctionType
AX = mybir.AxisListType.X
F32, F16, BF16 = mybir.dt.float32, mybir.dt.float16, mybir.dt.bfloat16

B, N, D = 4, 1024, 128
HEADS, DH, ROT = 16, 64, 32
FF, RANK = 512, 32
P = 128
TILES = B * N // P
KT = N // P
GH = 4
GROUPS = B * HEADS // GH
GPB = HEADS // GH
QW = 256
SLOTS = GH * N // QW
VW = 2 * DH + 1
VP = VW + 1
WSCALE = 16.0
MSCALE = 4096.0
EXP_SCALE = DH ** -0.5 / (WSCALE * WSCALE)
EPS = 1e-5
UNITS = 16
HALF = 8
FOLDS = 4
HAND = 6 * 16
PV_LAG = 5
LEAD = 24

PROJ_AT = [(3, 3), (4, 0), (4, 1), (4, 3), (5, 0), (5, 1), (5, 3), (6, 0), (6, 1), (6, 3), (7, 0), (7, 3),
           (8, 0), (8, 1), (8, 3), (9, 0)]
PROJ = [(w, c, t) for w in "qk" for c in range(2) for t in ("rot", "swap", "pass")] + [("v", c, "v") for c in range(4)]
OUT_AT = {(4, 2): ("turn", 1, 0), (5, 2): ("turn", 1, 1), (6, 2): ("out", 1, 0), (8, 2): ("out", 1, 1),
          (12, 0): ("turn", 0, 0), (12, 2): ("turn", 0, 1), (13, 0): ("out", 0, 0), (13, 2): ("out", 0, 1)}
MAX_AT = [(3, 2), (7, 2), (11, 2), (15, 2)]
HAND_ORDER = [("qk", 3), ("v", 3), ("qk", 0), ("qk", 1), ("v", 0), ("v", 1), ("qk", 2), ("v", 2)]


def tiles_of(first, last):
    out = []
    for k in range(SLOTS):
        for s in range(4):
            if (k, s) in PROJ_AT and not last:
                out.append((k, s, "proj", PROJ[PROJ_AT.index((k, s))]))
            if (k, s) in OUT_AT:
                kind, chunk, half = OUT_AT[k, s]
                if not (first and chunk == 1):
                    out.append((k, s, kind, (chunk, half)))
            if (k, s) in MAX_AT and not (last and k == SLOTS - 1):
                out += [(k, s, "max", (MAX_AT.index((k, s)), half)) for half in range(2)]
    return out


PRE_TILES = len(PROJ) + 2
FIRST_TILES = len(tiles_of(True, False))
MID_TILES = len(tiles_of(False, False))
assert PRE_TILES % 2 == 0 and FIRST_TILES % 2 == 0 and MID_TILES % 2 == 0


class Iteration:

    def __init__(self, i, first=False, last=False):
        self.i, self.first, self.last = i, first, last
        self.tiles = tiles_of(first, last)
        self.tile0 = PRE_TILES if first else PRE_TILES + FIRST_TILES + (i - 1) * MID_TILES

    def slot(self, k):
        return self.i * SLOTS + k

    def at(self, k, s):
        return [(n, t[2], t[3]) for n, t in enumerate(self.tiles) if t[:2] == (k, s)]

    def back(self, k, s, by):
        p = 4 * k + s - by
        return self.at(p // 4, p % 4) if p >= 0 else []


def build(nc, x_d, wq_d, wkv_d, wout_d, bout_d, u1_d, v1_d, b1_d, u2_d, v2_d, b2_d, rope_d, ident_d, out_d):
    with ExitStack() as ctx:
        def sb(name, shape, dt):
            return ctx.enter_context(nc.sbuf_tensor(name, shape, dt))

        def pb(name, shape, dt):
            return ctx.enter_context(nc.psum_tensor(name, shape, dt))

        def sem(name):
            return ctx.enter_context(nc.semaphore(name))

        X = sb("X", [P, TILES, D], F32)
        XT = sb("XT", [P, 2, B * N], F16)
        WQK = sb("WQK", [P, 2, 2, 3, HEADS * ROT], F16)
        WV = sb("WV", [P, 2, HEADS * DH], F16)
        WO = sb("WO", [P, HEADS * DH // P, D], F32)
        ROPE = sb("ROPE", [P, 2, N], F32)
        IDENT = sb("IDENT", [P, P], F32)
        IDENT16 = sb("IDENT16", [P, P], F16)
        BO = sb("BO", [P, D], F32)
        B2 = sb("B2", [P, D], F32)
        B1 = sb("B1", [P, FF // P], F32)
        B1R = sb("B1R", [FF // P, P], F32)
        U1 = sb("U1", [P, RANK], F32)
        V1 = sb("V1", [RANK, FF], F32)
        U2 = sb("U2", [P, FF // P, RANK], F32)
        V2 = sb("V2", [RANK, D], F32)
        WRAW = sb("WRAW", [P, 3, HEADS * DH], F32)
        QK = sb("QK", [P, GH, 4, N], F16)
        KHH = QK[:, :, 0, :]
        KL1 = QK[:, :, 1, :]
        QHL = QK[:, :, 2, :]
        QHM = QK[:, :, 3, :]
        V = sb("V", [P, GH, KT * VP], F16)
        STAGE = sb("STAGE", [P, 4, 2, N], F16)
        KS, QS = STAGE[:, 0:2, :, :], STAGE[:, 2:4, :, :]
        VS = sb("VS", [P, GH, KT * VP], F16)
        T1 = sb("T1", [P, 512], F32)
        T2 = sb("T2", [P, 512], F32)
        YR = sb("YR", [P, 512], F32)
        PF = sb("PF", [P, 4, 1024], F32)
        PR = sb("PR", [P, 4, 1024], F16)
        OS = sb("OS", [P, 2, 2, VW], F32)
        ON = sb("ON", [P, 2, DH], F32)
        RS = sb("RS", [P, 2, 1], F32)
        MINUS_ONE = sb("MINUS_ONE", [P, 2, 1], F32)
        OG = sb("OG", [P, 2, KT, P], F32)
        OT = sb("OT", [P, N], F32)
        MS = sb("MS", [P, 2, HALF // 2, N], F16)
        MN = sb("MN", [P, 2, KT], F16)
        ST = sb("ST", [P, TILES, 6], F32)
        MV = sb("MV", [P, TILES, 2], F32)
        VE = sb("VE", [P, TILES], F32)
        MINUS_HALF = sb("MINUS_HALF", [P, TILES], F32)
        RSTD = sb("RSTD", [P, TILES], F32)
        XN = PF[:, :, :].rearrange("p a (t d) -> p (a t) d", d=D)
        XT2, PT2, QT2, _ = (QK[:, h, :, :].rearrange("p a b -> p (a b)").bitcast(F32) for h in range(GH))
        HG, HG2 = (STAGE[:, a:a + 2, :, :].rearrange("p a b c -> p (a b c)").bitcast(F32) for a in (0, 2))

        S = [pb(f"S{n}", [P, 2, QW], F32) for n in range(2)]
        M = [pb(f"M{n}", [P, 512], F32) for n in range(2)]
        O = [pb(f"O{n}", [P, 2, 256], F32) for n in range(2)]
        T = [pb(f"TILE{n}", [P, 512], F32) for n in range(2)]

        x_in = [sem(f"x_in{b}") for b in range(B)]
        w_in, wo_in, small_in, rope_in = sem("w_in"), sem("wo_in"), sem("small_in"), sem("rope_in")
        stats, aggr, var_eps, rstd, xn_made = (sem(n) for n in ("stats", "aggr", "var_eps", "rstd", "xn_made"))
        xt_made, xt_hi, xt_lo = sem("xt_made"), sem("xt_hi"), sem("xt_lo")
        w_hi, w_lo, w_swap, set_up, bias_in = sem("w_hi"), sem("w_lo"), sem("w_swap"), sem("set_up"), sem("bias_in")
        tile_made = sem("tile_made")
        rot_read, rot_sum, rot_hi, rot_lo = sem("rot_read"), sem("rot_sum"), sem("rot_hi"), sem("rot_lo")
        pass_hi, pass_lo, v_hi, v_lo = sem("pass_hi"), sem("pass_lo"), sem("v_hi"), sem("v_lo")
        turned, added, max_row = sem("turned"), sem("added"), sem("max_row")
        handed = [sem(f"handed{h}") for h in range(GH)]
        v_handed = [sem(f"v_handed{h}") for h in range(GH)]
        unit_made, unit_copied, folded, max_found = (sem(n) for n in ("unit_made", "unit_copied", "folded", "max_found"))
        scored, exped, rest_made = sem("scored"), sem("exped"), sem("rest_made")
        pv_done, o_copied, o_sum, normed = sem("pv_done"), sem("o_copied"), sem("o_sum"), sem("normed")
        f_stats, f_aggr, f_xn = sem("f_stats"), sem("f_aggr"), sem("f_xn")
        f_turn, f_xt, f_p, f_pc, f_h, f_g, f_q, f_qc, f_y, f_out = (
            sem(f"f_{n}") for n in ("turn", "xt", "p", "pc", "h", "g", "q", "qc", "y", "out"))
        f_bias, stored = sem("f_bias"), sem("stored")
        powers_set = sem("powers_set")
        b1_turned, b1_copied = sem("b1_turned"), sem("b1_copied")

        def wait(e, s, value):
            if not (isinstance(value, int) and value <= 0):
                e.wait_ge(s, value)

        def freed(kind, args, it):
            if kind == "proj":
                w, c, t = args
                g = it.i + 1
                if t in ("rot", "swap"):
                    return rot_read, g * 8 + ("qk".index(w) * 2 + c) * 2 + (t == "swap") + 1
                if t == "pass":
                    return pass_lo, g * 4 + "qk".index(w) * 2 + c + 1
                return v_lo, g * 4 + c + 1
            if kind == "max":
                return max_row, (it.i * GH + 1 + args[0]) * 2 + args[1] + 1
            chunk, half = args
            nth = (it.i * 2 - chunk) * 2 + half + 1
            return (turned if kind == "turn" else added), nth

        def before(it, n):
            if n >= 2:
                return it.tiles[n - 2][2:], it
            if it.first:
                return [("proj", PROJ[-2 + n]), ("max", (-1, n))][1], it
            return Iteration(it.i - 1).tiles[n - 2][2:], Iteration(it.i - 1)

        def proj_tile(e, args, g, bank):
            w, c, t = args
            gi, b = g % GPB, g // GPB
            if w == "v":
                for r in range(2):
                    rows = bass.ds(b * N + (2 * c + r) * P, P)
                    cols = bass.ds(gi * GH * DH, GH * DH)
                    for n, (xp, wp) in enumerate(((0, 0), (0, 1), (1, 0))):
                        mm = e.matmul(T[bank][:, r * 256:(r + 1) * 256], XT[:, xp, rows], WV[:, wp, cols],
                                      start=(n == 0), stop=(n == 2))
            else:
                rows, cols = bass.ds(b * N + c * 512, 512), bass.ds(gi * GH * ROT, GH * ROT)
                kind = ("rot", "swap", "pass").index(t)
                for n, (xp, wp) in enumerate(((0, 0), (0, 1), (1, 0))):
                    mm = e.matmul(T[bank][:, :], WQK[:, "qk".index(w), wp, kind, cols], XT[:, xp, rows],
                                  start=(n == 0), stop=(n == 2))
            mm.then_inc(tile_made, 1)

        def max_tile(e, head, side, half, bank):
            if half == 0:
                e.wait_ge(max_found, 2 * head + 2)
            for j in range(4):
                mm = e.matmul(T[bank][DH:DH + 1, j * P:(j + 1) * P], MN[:, side, half * 4 + j:half * 4 + j + 1],
                              IDENT16[:, :], start=True, stop=True)
            mm.then_inc(tile_made, 1)

        def turn_tile(e, chunk, half, bank):
            for j in range(4):
                mm = e.transpose(T[bank][:, j * P:(j + 1) * P], OG[:, chunk, half * 4 + j, :], IDENT[:, :])
            mm.then_inc(tile_made, 1)

        def out_tile(e, chunk, half, bank, pair):
            for j in range(4):
                q = half * 4 + j
                mm = e.matmul(T[bank][:, j * P:(j + 1) * P], OT[:, q * P:(q + 1) * P], WO[:, pair, :],
                              start=True, stop=True)
            mm.then_inc(tile_made, 1)

        def pe_tiles(e, it, k, s):
            for n, kind, args in it.at(k, s):
                (kind0, args0), it0 = before(it, n)
                e.wait_ge(*freed(kind0, args0, it0))
                bank = n % 2
                if kind == "proj":
                    proj_tile(e, args, it.i + 1, bank)
                elif kind == "max":
                    max_tile(e, it.i * GH + 1 + args[0], (1 + args[0]) % 2, args[1], bank)
                elif kind == "turn":
                    chunk, half = args
                    e.wait_ge(normed, it.slot(8 if chunk == 0 else 0))
                    turn_tile(e, chunk, half, bank)
                else:
                    chunk, half = args
                    e.wait_ge(*freed("turn", (chunk, 1), it))
                    out_tile(e, chunk, half, bank, ((it.i - chunk) % GPB) * 2 + chunk)

        def pe_scores(e, it, k, s):
            n, h, quarter = it.slot(k), k // 4, k % 4
            if quarter == 0 and s == 0:
                e.wait_ge(max_row, (it.i * GH + h) * 2 + 2)
            wait(e, exped, 4 * n + s - 1)
            for kk in range(2):
                keys = slice((2 * s + kk) * P, (2 * s + kk + 1) * P)
                rows = slice(quarter * QW, (quarter + 1) * QW)
                e.matmul(S[s % 2][:, kk, :], KHH[:, h, keys], QHL[:, h, rows], start=True, stop=False)
                mm = e.matmul(S[s % 2][:, kk, :], KL1[0:DH + 1, h, keys], QHM[0:DH + 1, h, rows],
                              start=False, stop=True)
            mm.then_inc(scored, 1)

        def pe_values(e, n, k, s, fills):
            qt, half, h, bank = s % 2, s // 2, (k % SLOTS) // 4, k % 2
            if s == 0:
                wait(e, o_copied, n - 1)
                if k % 4 == 0:
                    e.wait_ge(v_handed[h], 16 * (fills + 1))
            if qt == 0:
                e.wait_ge(rest_made, 2 * n + half + 1)
            buf = (2 * k + half) % 4
            hi = PF[:, buf, :].bitcast(BF16)
            for j in range(4):
                kt = half * 4 + j
                at = j * QW + qt * P
                vals = V[:, h, kt * VP:kt * VP + VW]
                e.matmul(O[bank][:, qt, 0:VW], hi[:, 2 * at + 1:2 * (at + P):2], vals,
                         start=(s == 0 and j == 0), stop=False, skip_group_check=True)
                mm = e.matmul(O[bank][:, qt, 0:VW], PR[:, buf, at:at + P], vals,
                              start=False, stop=(half == 1 and j == 3), skip_group_check=True)
            if qt == 1:
                mm.then_inc(pv_done, 1)

        def pe_slot(e, it, k):
            for s in range(4):
                back = 4 * k + s - PV_LAG
                if not it.first or back >= 0:
                    pe_values(e, it.slot(back // 4), back // 4, back % 4, it.i)
                pe_tiles(e, it, k, s)
                pe_scores(e, it, k, s)
                if not (it.last and 4 * k + LEAD + s >= GH * UNITS):
                    place_u = 4 * k + LEAD + s
                    fills = it.i + place_u // (GH * UNITS) + 1
                    u = it.slot(k) * 4 + LEAD + s
                    place, unit = (place_u // UNITS) % GH, place_u % UNITS
                    if unit == 0:
                        e.wait_ge(handed[place], HAND * fills)
                    e.wait_ge(unit_copied, u - 1)
                    e.matmul(M[s % 2][:, :], QHL[:, place, (unit // 2) * P:(unit // 2 + 1) * P],
                             KHH[:, place, (unit % 2) * 512:(unit % 2 + 1) * 512],
                             start=True, stop=True).then_inc(unit_made, 1)

        def act_tile(e, kind, args, made, g, bank):
            if kind == "proj" and args[2] == "pass":
                w, c, _ = args
                st = (QS, KS)["qk".index(w)]
                e.wait_ge(tile_made, made)
                if w == "q" and c == 0:
                    for h in range(GH):
                        wait(e, handed[h], HAND * g)
                e.activation(st[:, 0, 1, c * 512:(c + 1) * 512], T[bank][:, :], ACT.Copy).then_inc(pass_hi, 1)
            elif kind == "proj" and args[2] == "v":
                c = args[1]
                e.wait_ge(tile_made, made)
                if c == 0:
                    for h in range(GH):
                        wait(e, v_handed[h], 16 * g)
                for r in range(2):
                    dst = VS[:, :, :].rearrange("p h (t v) -> p h t v", v=VP)[:, :, 2 * c + r, 0:DH]
                    src = T[bank][:, r * 256:(r + 1) * 256].rearrange("p (h d) -> p h d", d=DH)
                    cp = e.activation(dst, src, ACT.Copy)
                cp.then_inc(v_hi, 1)

        def act_rot(e, args, g):
            w, c, _ = args
            st, nth = (QS, KS)["qk".index(w)], "qk".index(w) * 2 + c
            e.wait_ge(rot_sum, g * 4 + nth + 1)
            if nth == 0:
                for h in range(GH):
                    wait(e, handed[h], HAND * g)
            e.activation(st[:, 0, 0, c * 512:(c + 1) * 512], YR[:, :], ACT.Copy).then_inc(rot_hi, 1)

        def act_max(e, head, place, half, made, bank):
            e.wait_ge(tile_made, made)
            e.activation(QHM[DH:DH + 1, place, half * 512:(half + 1) * 512], T[bank][DH:DH + 1, :],
                         ACT.Copy).then_inc(max_row, 1)

        def act_tiles(e, it, k, s):
            for n, kind, args in it.at(k, s):
                made, bank = it.tile0 + n + 1, n % 2
                if kind == "proj":
                    act_tile(e, kind, args, made, it.i + 1, bank)
                elif kind == "max":
                    if args[1] == 0:
                        wait(e, scored, (it.i * GH + 1 + args[0]) * 16 - 48)
                    act_max(e, None, (1 + args[0]) % GH, args[1], made, bank)
                elif kind == "turn":
                    e.wait_ge(tile_made, made)
                    e.activation(OT[:, args[1] * 512:(args[1] + 1) * 512], T[bank][:, :], ACT.Copy).then_inc(turned, 1)
            for n, kind, args in it.back(k, s, 3):
                if kind == "proj" and args[2] == "swap":
                    act_rot(e, args, it.i + 1)

        def act_copy_out(e, n, k):
            e.wait_ge(pv_done, 2 * n + 2)
            wait(e, normed, n - 1)
            e.activation(OS[:, k % 2, :, :], O[k % 2][:, :, 0:VW], ACT.Copy).then_inc(o_copied, 1)

        def act_unit(e, u, half, place_u):
            e.wait_ge(unit_made, u + 1)
            if place_u % HALF == 0:
                wait(e, max_found, half - 1)
            q, c = (place_u % HALF) // 2, place_u % 2
            e.activation(MS[:, (place_u // HALF) % 2, q, c * 512:(c + 1) * 512], M[place_u % 2][:, :], ACT.Copy,
                         scale=-1.0 / MSCALE).then_inc(unit_copied, 1)

        def act_slot(e, it, k):
            n = it.slot(k)
            for s in range(4):
                place_u = 4 * k + s + LEAD - 1
                if not (it.last and place_u >= GH * UNITS):
                    act_unit(e, 4 * n + s + LEAD - 1, it.i * (GH * UNITS // HALF) + place_u // HALF, place_u)
                if s == 1 and (not it.first or k >= 2):
                    act_copy_out(e, it.slot(k - 2), k)
                act_tiles(e, it, k, s)
                e.wait_ge(scored, 4 * n + s + 1)
                if s % 2 == 0:
                    wait(e, pv_done, 2 * n - 3 + s // 2)
                e.activation(PF[:, (2 * k + s // 2) % 4, (s % 2) * 512:(s % 2 + 1) * 512],
                             S[s % 2][:, :, :].rearrange("p a b -> p (a b)"), ACT.Exp,
                             scale=EXP_SCALE).then_inc(exped, 1)

        def dve_tile(e, kind, args, made, g, bank):
            w, c, t = args
            nth = "qkv".index(w) * 2 + c
            cols = slice(c * 512, (c + 1) * 512)
            if t in ("rot", "swap"):
                e.wait_ge(tile_made, made)
                if t == "rot":
                    wait(e, rot_sum, g * 4 + nth)
                e.tensor_tensor((T1, T2)[t == "swap"][:, :], T[bank][:, :], ROPE[:, int(t == "swap"), cols],
                                ALU.mult).then_inc(rot_read, 1)
            elif t == "pass":
                st = (QS, KS)["qk".index(w)]
                e.wait_ge(pass_hi, g * 4 + nth + 1)
                e.tensor_tensor(st[:, 1, 1, cols], T[bank][:, :], st[:, 0, 1, cols], ALU.subtract).then_inc(pass_lo, 1)
            else:
                e.wait_ge(v_hi, g * 4 + c + 1)
                vs = VS[:, :, :].rearrange("p h (t v) -> p h t v", v=VP)
                for r in range(2):
                    src = T[bank][:, r * 256:(r + 1) * 256].rearrange("p (h d) -> p h d", d=DH)
                    tt = e.tensor_tensor(vs[:, :, 2 * c + r, DH:2 * DH], src, vs[:, :, 2 * c + r, 0:DH], ALU.subtract)
                tt.then_inc(v_lo, 1)

        def dve_tiles(e, it, k, s):
            for n, kind, args in it.back(k, s, 1):
                made, bank = it.tile0 + n + 1, n % 2
                if kind == "proj":
                    dve_tile(e, kind, args, made, it.i + 1, bank)
                elif kind == "out":
                    chunk, half = args
                    b = (it.i - chunk) // GPB
                    e.wait_ge(tile_made, made)
                    xs = X[:, bass.ds(b * KT + half * 4, 4), :]
                    e.tensor_tensor(xs, T[bank][:, :].rearrange("p (t d) -> p t d", d=D), xs, ALU.add).then_inc(added, 1)

        def dve_fold(e, half, place, part):
            ms = MS[:, place % 2, :, :]
            if part == 0:
                e.wait_ge(unit_copied, (half + 1) * HALF)
            for level in ((0,), (1, 2), (3,))[part]:
                w = N // 2 >> level
                if level:
                    e.wait_ge(folded, half * FOLDS + level)
                e.tensor_tensor(ms[:, :, 0:w], ms[:, :, 0:w], ms[:, :, w:2 * w], ALU.min).then_inc(folded, 1)
            if part == 2:
                e.wait_ge(folded, (half + 1) * FOLDS)
                e.tensor_reduce(MN[:, (place // 2) % 2, (place % 2) * 4:(place % 2) * 4 + 4], ms[:, :, 0:w], AX,
                                ALU.min).then_inc(max_found, 1)

        def dve_rest(e, n, k, pair):
            buf = (2 * k + pair) % 4
            e.wait_ge(exped, 4 * n + 2 * pair + 2)
            e.tensor_tensor(PR[:, buf, :], PF[:, buf, :], PF[:, buf, :].bitcast(BF16)[:, 1:2048:2],
                            ALU.subtract).then_inc(rest_made, 1)

        def dve_slot(e, it, k):
            n = it.slot(k)
            for s in range(4):
                dve_tiles(e, it, k, s)
                if s == 0 and (not it.first or k > 0):
                    dve_rest(e, it.slot(k - 1), k - 1, 1)
                if s == 2:
                    dve_rest(e, n, k, 0)
                for part in range(3):
                    place_u = 4 * k + s + LEAD - 2 - part
                    if place_u % HALF == HALF - 1 and not (it.last and place_u >= GH * UNITS):
                        place = place_u // HALF
                        dve_fold(e, it.i * (GH * UNITS // HALF) + place, place, part)

        def pool_sum(e, args, g):
            w, c, _ = args
            nth = g * 4 + "qk".index(w) * 2 + c
            e.wait_ge(rot_read, nth * 2 + 2)
            wait(e, rot_lo, nth)
            e.tensor_tensor(YR[:, :], T1[:, :], T2[:, :], ALU.add).then_inc(rot_sum, 1)

        def pool_rot(e, args, g):
            w, c, _ = args
            st, nth = (QS, KS)["qk".index(w)], "qk".index(w) * 2 + c
            cols = slice(c * 512, (c + 1) * 512)
            e.wait_ge(rot_hi, g * 4 + nth + 1)
            e.tensor_tensor(st[:, 1, 0, cols], YR[:, :], st[:, 0, 0, cols], ALU.subtract).then_inc(rot_lo, 1)

        def pool_norm(e, n, k):
            h, side, q = (k % SLOTS) // 4, k % 2, (k % 4) * 2
            e.wait_ge(o_copied, n + 1)
            wait(e, normed, n)
            e.tensor_tensor(ON[:, :, :], OS[:, side, :, 0:DH], OS[:, side, :, DH:2 * DH], ALU.add).then_inc(o_sum, 1)
            e.tensor_tensor(RS[:, :, :], OS[:, side, :, 2 * DH:VW], MINUS_ONE[:, :, :], ALU.pow).then_inc(o_sum, 1)
            e.wait_ge(o_sum, 2 * n + 2)
            e.tensor_tensor(OG[:, h // 2, q:q + 2, (h % 2) * DH:(h % 2 + 1) * DH], ON[:, :, :],
                            RS[:, :, :].broadcast_to([P, 2, DH]), ALU.mult).then_inc(normed, 1)

        def pool_slot(e, it, k):
            for s in range(4):
                for n, kind, args in it.back(k, s, 1):
                    if kind == "proj" and args[2] == "swap":
                        pool_sum(e, args, it.i + 1)
                for n, kind, args in it.back(k, s, 4):
                    if kind == "proj" and args[2] == "swap":
                        pool_rot(e, args, it.i + 1)
                if s == 2 and (not it.first or k >= 2):
                    if k - 2 == 0 and not it.first:
                        e.wait_ge(*freed("turn", (0, 1), Iteration(it.i - 1)))
                    if k - 2 == 8 and not it.first:
                        e.wait_ge(*freed("turn", (1, 1), it))
                    pool_norm(e, it.slot(k - 2), k - 2)

        def hand_over(sp, what, h):
            rows = slice(32 * h, 32 * h + 32)
            if what == "v":
                sp.dma_start(V[:, h, :], VS[:, h, :]).then_inc(v_handed[h], 16)
                return
            for t in range(2):
                top, low = slice(32 * t, 32 * t + 32), slice(DH + 32 * t, DH + 32 * t + 32)
                sp.dma_start(QK[top, h, 0:2, :], STAGE[rows, 0:2, t, :]).then_inc(handed[h], 16)
                sp.dma_start(QK[top, h, 2:4, :], STAGE[rows, 2:3, t, :].broadcast_to([32, 2, N])).then_inc(handed[h], 16)
                sp.dma_start(QK[low, h, 0:3:2, :], STAGE[rows, 0:4:3, t, :]).then_inc(handed[h], 16)

        def sp_iteration(sp, it):
            for what, h in HAND_ORDER:
                if (it.first if h == GH - 1 else it.last):
                    continue
                if what == "v":
                    if h == 0:
                        sp.wait_ge(v_lo, (it.i + 1) * 4 + 4)
                    sp.wait_ge(pv_done, ((it.i - (h == GH - 1)) * 16 + 4 * h + 4) * 2)
                elif h == 0:
                    sp.wait_ge(rot_lo, (it.i + 1) * 4 + 4)
                    sp.wait_ge(pass_lo, (it.i + 1) * 4 + 4)
                else:
                    sp.wait_ge(scored, (it.i - (h == GH - 1)) * 64 + 16 * h + 16)
                hand_over(sp, what, h)

        block = ctx.enter_context(nc.Block())

        def loop(e, body):
            body(e, Iteration(0, first=True))
            with e.Fori(1, GROUPS - 1) as i:
                body(e, Iteration(i))
            body(e, Iteration(GROUPS - 1, last=True))

        END = GROUPS * SLOTS
        end = Iteration(GROUPS)
        FC = B * N // 512
        tail0 = PRE_TILES + FIRST_TILES + (GROUPS - 2) * MID_TILES + len(tiles_of(False, True))
        assert tail0 % 2 == 0

        @block.sync
        def _(sp):
            xr = x_d.rearrange("b (t p) d -> p (b t) d", p=P)
            sp.dma_start(X[:, 0:KT, :], xr[:, 0:KT, :]).then_inc(x_in[0], 16)
            sp.dma_start(IDENT[:, :], ident_d).then_inc(rope_in, 16)
            sp.dma_start(WRAW[:, 1:3, :], wkv_d.rearrange("p (a n) -> p a n", a=2)).then_inc(w_in, 16)
            sp.dma_start(ROPE[:, :, :], rope_d.rearrange("p (a n) -> p a n", a=2)).then_inc(rope_in, 16)
            for b in range(1, B):
                sp.dma_start(X[:, b * KT:(b + 1) * KT, :], xr[:, b * KT:(b + 1) * KT, :]).then_inc(x_in[b], 16)
            sp.dma_start(WO[:, :, :], wout_d.rearrange("(c p) n -> p c n", p=P)).then_inc(wo_in, 16)
            sp.wait_ge(rot_lo, 4)
            sp.wait_ge(pass_lo, 4)
            sp.wait_ge(set_up, 3)
            for h in range(GH):
                hand_over(sp, "qk", h)
            sp.wait_ge(v_lo, 4)
            for h in range(GH):
                hand_over(sp, "v", h)
            loop(sp, sp_iteration)
            for c in range(FC):
                sp.wait_ge(f_out, c + 1)
                sp.dma_start(out_d.rearrange("b (t p) d -> p (b t) d", p=P)[:, 4 * c:4 * c + 4, :],
                             X[:, 4 * c:4 * c + 4, :]).then_inc(stored, 16)
            sp.wait_ge(stored, 16 * FC)

        @block.gpsimd
        def _(pool):
            def take_rstd(nth, t0, t1):
                pool.wait_ge(var_eps, nth + 1)
                pool.tensor_tensor(RSTD[:, t0:t1], VE[:, t0:t1], MINUS_HALF[:, t0:t1], ALU.pow).then_inc(rstd, 1)

            pool.memset(MINUS_HALF[:, :], -0.5).then_inc(powers_set, 1)
            pool.memset(MINUS_ONE[:, :, :], -1.0).then_inc(powers_set, 1)
            pool.wait_ge(powers_set, 2)
            take_rstd(0, 0, KT)
            pool.wait_ge(rstd, 1)
            pool.memset(QK[DH:DH + 32, :, 1, :], MSCALE).then_inc(set_up, 1)
            pool.wait_ge(set_up, 1)
            pool.memset(VS[:, :, :].rearrange("p h (t v) -> p h t v", v=VP)[:, :, :, 2 * DH:VP], WSCALE).then_inc(set_up, 1)
            pool.wait_ge(rope_in, 32)
            pool.tensor_copy(IDENT16[:, :], IDENT[:, :]).then_inc(set_up, 1)
            for w in range(2):
                pool.wait_ge(w_lo, 2 * w + 1)
                pair = WQK[:, w, :, 0, :].rearrange("p a (n e) -> p a n e", e=2)
                swap = WQK[:, w, :, 1, :].rearrange("p a (n e) -> p a n e", e=2)
                pool.tensor_scalar(swap[:, :, :, 0], pair[:, :, :, 1], -1.0, None, ALU.mult).then_inc(w_swap, 1)
                pool.tensor_copy(swap[:, :, :, 1], pair[:, :, :, 0]).then_inc(w_swap, 1)
            for args in PROJ:
                if args[2] == "pass":
                    pool_sum(pool, args, 0)
                    pool_rot(pool, args, 0)
            for b in range(1, B):
                take_rstd(b, b * KT, (b + 1) * KT)
            pool.wait_ge(small_in, 16 * 7)
            for b in range(B):
                pool.wait_ge(xn_made, b + 1)
                for t in range(KT):
                    xs = X[:, b * KT + t, :]
                    tt = pool.tensor_tensor(xs, xs, BO[:, :], ALU.add)
                tt.then_inc(bias_in, 1)

            def body(e, it):
                for k in range(SLOTS):
                    pool_slot(e, it, k)

            loop(pool, body)
            pool_norm(pool, END - 2, SLOTS - 2)
            pool_norm(pool, END - 1, SLOTS - 1)
            take_rstd(B, 0, TILES)

        @block.scalar
        def _(act):
            act.dma_start(WRAW[:, 0, :], wq_d).then_inc(w_in, 16)
            act.dma_start(BO[:, :], bout_d.rearrange("(a n) -> a n", a=1).broadcast_to([P, D])).then_inc(small_in, 16)
            act.dma_start(B2[:, :], b2_d.rearrange("(a n) -> a n", a=1).broadcast_to([P, D])).then_inc(small_in, 16)
            act.dma_start(B1R[:, :], b1_d.rearrange("(c p) -> c p", p=P)).then_inc(small_in, 16)
            act.dma_start(U1[:, :], u1_d).then_inc(small_in, 16)
            act.dma_start(V1[:, :], v1_d).then_inc(small_in, 16)
            act.dma_start(U2[:, :, :], u2_d.rearrange("(c p) r -> p c r", p=P)).then_inc(small_in, 16)
            act.dma_start(V2[:, :], v2_d).then_inc(small_in, 16)

            def w_part(w):
                if w < 2:
                    src = WRAW[:, w, :].rearrange("p (h d) -> p h d", d=DH)
                    for kind, d0 in ((0, 0), (2, ROT)):
                        act.activation(WQK[:, w, 0, kind, :].rearrange("p (h d) -> p h d", d=ROT),
                                       src[:, :, d0:d0 + ROT], ACT.Copy, scale=WSCALE).then_inc(w_hi, 1)
                else:
                    act.activation(WV[:, 0, :], WRAW[:, 2, :], ACT.Copy, scale=WSCALE).then_inc(w_hi, 1)

            def xt_part(c):
                act.wait_ge(xt_made, c + 1)
                act.activation(XT[:, 0, c * 512:(c + 1) * 512], S[c % 2][:, :, :].rearrange("p a b -> p (a b)"),
                               ACT.Copy).then_inc(xt_hi, 1)

            act.wait_ge(w_in, 32)
            for w in range(3):
                w_part(w)
            xt_part(0)
            xt_part(1)
            for n, args in enumerate(PROJ):
                act_tile(act, "proj", args, n + 1, 0, n % 2)
                if args[2] == "pass":
                    act_rot(act, args, 0)
            for c in range(2, 8):
                xt_part(c)
            act.wait_ge(b1_turned, 1)
            act.activation(B1[:, :], M[0][:, 0:FF // P], ACT.Copy).then_inc(b1_copied, 1)
            for u in range(LEAD - 1):
                act_unit(act, u, u // HALF, u)
                if u == UNITS + 2:
                    for half in range(2):
                        act_max(act, 0, 0, half, len(PROJ) + half + 1, half)

            def body(e, it):
                for k in range(SLOTS):
                    act_slot(e, it, k)

            loop(act, body)
            act_copy_out(act, END - 2, SLOTS - 2)
            act_copy_out(act, END - 1, SLOTS - 1)
            for half in range(2):
                act.wait_ge(tile_made, tail0 + half + 1)
                act.activation(OT[:, half * 512:(half + 1) * 512], T[half][:, :], ACT.Copy).then_inc(turned, 1)
            for c in range(FC):
                act.wait_ge(f_turn, c + 1)
                act.activation(XT2[:, (c % 4) * 512:(c % 4 + 1) * 512], M[0][:, :], ACT.Copy).then_inc(f_xt, 1)
                for f in range(4):
                    act.wait_ge(f_h, 4 * c + f + 1)
                    if f == 0:
                        wait(act, f_q, c - 1)
                    act.activation((HG, HG2)[c % 2][:, f * 512:(f + 1) * 512],
                                   S[f % 2][:, :, :].rearrange("p a b -> p (a b)"), ACT.Gelu_apprx_tanh,
                                   bias=B1[:, f:f + 1]).then_inc(f_g, 1)

        @block.tensor
        def _(pe):
            def turn_x(c):
                pe.wait_ge(xn_made, c // 2 + 1)
                if c == 0:
                    pe.wait_ge(rope_in, 32)
                wait(pe, xt_lo, c - 1)
                for j in range(4):
                    mm = pe.transpose(S[c % 2][:, :, :].rearrange("p a b -> p (a b)")[:, j * P:(j + 1) * P],
                                      XN[:, c * 4 + j, :], IDENT[:, :])
                mm.then_inc(xt_made, 1)

            turn_x(0)
            turn_x(1)
            pe.wait_ge(xt_lo, 2)
            pe.wait_ge(w_swap, 4)
            pe.wait_ge(w_lo, 5)
            pre = Iteration(-1)
            for n, args in enumerate(PROJ):
                if n >= 2:
                    pe.wait_ge(*freed("proj", PROJ[n - 2], pre))
                proj_tile(pe, args, 0, n % 2)
            for c in range(2, 8):
                turn_x(c)
            pe.wait_ge(small_in, 16 * 7)
            pe.transpose(M[0][:, 0:FF // P], B1R[:, :], IDENT[0:FF // P, 0:FF // P]).then_inc(b1_turned, 1)
            pe.wait_ge(b1_copied, 1)
            pe.wait_ge(set_up, 3)
            for u in range(LEAD):
                if u % UNITS == 0:
                    pe.wait_ge(handed[u // UNITS], HAND)
                wait(pe, unit_copied, u - 1)
                unit = u % UNITS
                pe.matmul(M[u % 2][:, :], QHL[:, u // UNITS, (unit // 2) * P:(unit // 2 + 1) * P],
                          KHH[:, u // UNITS, (unit % 2) * 512:(unit % 2 + 1) * 512],
                          start=True, stop=True).then_inc(unit_made, 1)
                if u == UNITS + 2:
                    for half in range(2):
                        pe.wait_ge(*freed("proj", PROJ[len(PROJ) - 2 + half], pre))
                        max_tile(pe, 0, 0, half, half)
            pe.wait_ge(xt_lo, 8)

            def body(e, it):
                for k in range(SLOTS):
                    if k == 4 and it.first:
                        e.wait_ge(wo_in, 16)
                    pe_slot(e, it, k)

            loop(pe, body)
            for back in range(4 * SLOTS - PV_LAG, 4 * SLOTS):
                pe_values(pe, END - SLOTS + back // 4, back // 4, back % 4, GROUPS - 1)
            pe.wait_ge(normed, END)
            lastit = Iteration(GROUPS - 1, last=True)
            for half in range(2):
                kind, args = lastit.tiles[half - 2][2:]
                pe.wait_ge(*freed(kind, args, lastit))
                turn_tile(pe, 1, half, half)
            pe.wait_ge(turned, GROUPS * 4)
            for half in range(2):
                out_tile(pe, 1, half, half, HEADS // 2 - 1)
            pe.wait_ge(unit_copied, 64 * UNITS)
            pe.wait_ge(exped, 4 * END)

            def part_a(c):
                pe.wait_ge(f_xn, c + 1)
                wait(pe, f_xt, c)
                for j in range(4):
                    mm = pe.transpose(M[0][:, j * P:(j + 1) * P], XN[:, (4 * c + j) % 32, :], IDENT[:, :])
                mm.then_inc(f_turn, 1)
                pe.wait_ge(f_xt, c + 1)
                wait(pe, f_pc, c)
                pe.matmul(M[1][0:RANK, :], U1[:, :], XT2[:, (c % 4) * 512:(c % 4 + 1) * 512],
                          start=True, stop=True).then_inc(f_p, 1)

            def part_b(c):
                pe.wait_ge(f_pc, c + 1)
                for f in range(4):
                    wait(pe, f_g, 4 * c + f - 1)
                    pe.matmul(S[f % 2][:, :, :].rearrange("p a b -> p (a b)"), V1[:, f * P:(f + 1) * P],
                              PT2[0:RANK, (c % 4) * 512:(c % 4 + 1) * 512], start=True, stop=True).then_inc(f_h, 1)

            def part_c(c):
                wait(pe, f_qc, c)
                for f in range(4):
                    pe.wait_ge(f_g, 4 * c + f + 1)
                    mm = pe.matmul(O[0][0:RANK, :, :].rearrange("p a b -> p (a b)"), U2[:, f, :],
                                   (HG, HG2)[c % 2][:, f * 512:(f + 1) * 512], start=(f == 0), stop=(f == 3))
                mm.then_inc(f_q, 1)
                pe.wait_ge(f_qc, c + 1)
                wait(pe, f_out, c - 1) if c >= 2 else pe.wait_ge(added, GROUPS * 4)
                for j in range(4):
                    mm = pe.matmul(T[c % 2][:, j * P:(j + 1) * P],
                                   QT2[0:RANK, (c % 4) * 512 + j * P:(c % 4) * 512 + (j + 1) * P], V2[:, :],
                                   start=True, stop=True)
                mm.then_inc(f_y, 1)

            pe.wait_ge(o_copied, END)
            part_a(0)
            for c in range(FC):
                part_b(c)
                if c + 1 < FC:
                    part_a(c + 1)
                part_c(c)

        @block.vector
        def _(dve):
            def ln_stats(t0, t1, s1, s2, base):
                for t in range(t0, t1):
                    bs = dve.bn_stats(ST[:, t, :], X[:, t, :])
                bs.then_inc(s1, 1)
                dve.wait_ge(s1, base + 1)
                for t in range(t0, t1):
                    ba = dve.bn_aggr(MV[:, t, :], ST[:, t, :])
                ba.then_inc(s2, 1)
                dve.wait_ge(s2, base + 1)
                dve.tensor_scalar(VE[:, t0:t1], MV[:, t0:t1, 1], EPS, None, ALU.add).then_inc(var_eps, 1)

            def ln_apply(t0, t1, s):
                for t in range(t0, t1):
                    ts = dve.tensor_scalar(XN[:, t, :], X[:, t, :], MV[:, t, 0:1], RSTD[:, t:t + 1],
                                           ALU.subtract, ALU.mult)
                ts.then_inc(s, 1)

            def batch_stats(b):
                dve.wait_ge(x_in[b], 16)
                ln_stats(b * KT, (b + 1) * KT, stats, aggr, b)

            def batch_apply(b):
                dve.wait_ge(rstd, b + 1)
                ln_apply(b * KT, (b + 1) * KT, xn_made)

            def xt_part(c):
                dve.wait_ge(xt_hi, c + 1)
                cols = slice(c * 512, (c + 1) * 512)
                dve.tensor_tensor(XT[:, 1, cols], S[c % 2][:, :, :].rearrange("p a b -> p (a b)"), XT[:, 0, cols],
                                  ALU.subtract).then_inc(xt_lo, 1)

            batch_stats(0)
            batch_apply(0)
            dve.wait_ge(w_in, 32)
            for w in range(2):
                src = WRAW[:, w, :].rearrange("p (h d) -> p h d", d=DH)
                for n, (kind, d0) in enumerate(((0, 0), (2, ROT))):
                    dve.wait_ge(w_hi, 2 * w + n + 1)
                    hi, lo = (WQK[:, w, hl, kind, :].rearrange("p (h d) -> p h d", d=ROT) for hl in range(2))
                    dve.scalar_tensor_tensor(lo, src[:, :, d0:d0 + ROT], WSCALE, hi, ALU.mult,
                                             ALU.subtract).then_inc(w_lo, 1)
            xt_part(0)
            xt_part(1)
            dve.wait_ge(w_hi, 5)
            dve.scalar_tensor_tensor(WV[:, 1, :], WRAW[:, 2, :], WSCALE, WV[:, 0, :], ALU.mult,
                                     ALU.subtract).then_inc(w_lo, 1)
            for n, args in enumerate(PROJ):
                dve_tile(dve, "proj", args, n + 1, 0, n % 2)
            for b in range(1, B):
                batch_stats(b)
            for b in range(1, B):
                batch_apply(b)
                xt_part(2 * b)
                xt_part(2 * b + 1)
            for half in range(2):
                for part in range(3):
                    dve_fold(dve, half, half, part)

            def body(e, it):
                for k in range(SLOTS):
                    if it.first and k == 12:
                        e.wait_ge(bias_in, B)
                    dve_slot(e, it, k)

            loop(dve, body)
            dve_rest(dve, END - 1, SLOTS - 1, 1)
            for half in range(2):
                dve.wait_ge(tile_made, tail0 + 2 + half + 1)
                xs = X[:, (B - 1) * KT + half * 4:(B - 1) * KT + half * 4 + 4, :]
                dve.tensor_tensor(xs, T[half][:, :].rearrange("p (t d) -> p t d", d=D), xs, ALU.add).then_inc(added, 1)
            dve.wait_ge(added, GROUPS * 4)
            dve.wait_ge(pv_done, 2 * END)
            ln_stats(0, TILES, f_stats, f_aggr, 0)
            dve.wait_ge(rstd, B + 1)
            for c in range(FC):
                ln_apply(4 * c, 4 * c + 4, f_xn)
            dve.wait_ge(f_xn, FC)
            for t in range(TILES):
                tt = dve.tensor_tensor(X[:, t, :], X[:, t, :], B2[:, :], ALU.add)
            tt.then_inc(f_bias, 1)
            dve.wait_ge(f_bias, 1)

            def copy_p(c):
                dve.wait_ge(f_p, c + 1)
                dve.tensor_copy(PT2[0:RANK, (c % 4) * 512:(c % 4 + 1) * 512], M[1][0:RANK, :]).then_inc(f_pc, 1)

            copy_p(0)
            for c in range(FC):
                if c + 1 < FC:
                    copy_p(c + 1)
                dve.wait_ge(f_q, c + 1)
                dve.tensor_copy(QT2[0:RANK, (c % 4) * 512:(c % 4 + 1) * 512],
                                O[0][0:RANK, :, :].rearrange("p a b -> p (a b)")).then_inc(f_qc, 1)
                dve.wait_ge(f_y, c + 1)
                xs = X[:, 4 * c:4 * c + 4, :]
                dve.tensor_tensor(xs, T[c % 2][:, :].rearrange("p (t d) -> p t d", d=D), xs, ALU.add).then_inc(f_out, 1)


def rope_table():
    inv = np.float32(1.0) / np.float32(10000.0) ** (np.arange(0, ROT, 2, dtype=np.float32) / np.float32(ROT))
    ang = np.arange(N, dtype=np.float32)[:, None] * inv[None, :]
    both = [np.tile(np.repeat(f(ang).T, 2, axis=0), (GH, 1)) for f in (np.cos, np.sin)]
    return np.ascontiguousarray(np.concatenate(both, axis=1).astype(np.float32))


ROPE_TABLE = rope_table()
IDENTITY = np.eye(P, dtype=np.float32)

_INS = ["L0_attn_queries", "L0_attn_Wq", "L0_attn_Wkv", "L0_attn_Wout", "L0_attn_bout", "L0_ffn_U1", "L0_ffn_V1",
        "L0_ffn_b1", "L0_ffn_U2", "L0_ffn_V2", "L0_ffn_b2"]


def kernel(**inputs):
    import concourse.bacc as bacc
    from concourse.bass_utils import run_bass_kernel_spmd

    nc = bacc.Bacc("TRN2", target_bir_lowering=False, num_devices=1)
    arrays = {f"in_{n}": np.ascontiguousarray(inputs[n]) for n in _INS}
    arrays["in_rope"], arrays["in_ident"] = ROPE_TABLE, IDENTITY
    args = [nc.dram_tensor(n, a.shape, mybir.dt.from_np(a.dtype), kind="ExternalInput").ap() for n, a in arrays.items()]
    args.append(nc.dram_tensor("out", (B, N, D), F32, kind="ExternalOutput").ap())
    build(nc, *args)
    r = run_bass_kernel_spmd(nc, [arrays], core_ids=[0])
    return r.results[0]["out"]
```

```python
from contextlib import ExitStack

import numpy as np

import concourse.bass as bass
from concourse import mybir
from concourse.alu_op_type import AluOpType as ALU

ACT = mybir.ActivationFunctionType
AX = mybir.AxisListType.X
F32, F16, BF16 = mybir.dt.float32, mybir.dt.float16, mybir.dt.bfloat16

B, N, D = 4, 1024, 128
HEADS, DH, ROT = 16, 64, 32
FF, RANK = 512, 32
P = 128
TILES = B * N // P
KT = N // P
GH = 4
GROUPS = B * HEADS // GH
GPB = HEADS // GH
QW = 256
SLOTS = GH * N // QW
VW = 2 * DH + 1
VP = VW + 1
WSCALE = 16.0
MSCALE = 4096.0
EXP_SCALE = DH ** -0.5 / (WSCALE * WSCALE)
EPS = 1e-5
UNITS = 16
HALF = 8
FOLDS = 4
HAND = 6 * 16
PV_LAG = 5
LEAD = 24

CHUNK = 4
FC = TILES // CHUNK
EARLY = (B - 1) * KT // CHUNK
PROJ_AT = [(p // 4, p % 4) for p in (5, 8, 9, 11, 16, 20, 23, 25, 28, 32, 35, 37)]
PROJ = [(w, c, t) for w in "qk" for c in range(2) for t in ("rot", "pass")] + [("v", c, "v") for c in range(4)]
OUT_AT = {(4, 2): ("turn", 1, 0), (5, 2): ("turn", 1, 1), (6, 2): ("out", 1, 0), (8, 2): ("out", 1, 1),
          (12, 0): ("turn", 0, 0), (12, 2): ("turn", 0, 1), (13, 1): ("out", 0, 0), (14, 0): ("out", 0, 1)}
PRE_CHUNKS = KT // CHUNK
TURN_X0_AT = [(9, 3), (10, 0), (10, 2), (11, 0), (13, 3), (14, 3)]
STATS_AT = {3: 2, 11: 3}
APPLY_AT = [(8, 3), (9, 1), (10, 0), (10, 1), (12, 3), (13, 1)]
BIAS_AT = [(9, 3), (10, 3), (11, 1), (11, 3), (14, 2), (14, 3)]
TURN_X_AT = [(c + 2, 1) for c in range(EARLY)]
DOWN_AT = [(c + 3, 0) for c in range(EARLY)]
MAX_AT = {(4 * h + 3, 2 + half): (h, half) for h in range(GH) for half in range(2)}
HAND_ORDER = [("qk", 3), ("v", 3), ("qk", 0), ("qk", 1), ("v", 0), ("v", 1), ("qk", 2), ("v", 2)]


def tiles_of(first, last):
    out = []
    for k in range(SLOTS):
        for s in range(4):
            if (k, s) in PROJ_AT and not last:
                out.append((k, s, "proj", PROJ[PROJ_AT.index((k, s))]))
            if first and (k, s) in TURN_X0_AT:
                out.append((k, s, "turn_x", (0, PRE_CHUNKS + TURN_X0_AT.index((k, s)))))
            if last and (k, s) in TURN_X_AT:
                out.append((k, s, "turn_x", (1, TURN_X_AT.index((k, s)))))
            if last and (k, s) in DOWN_AT:
                out.append((k, s, "down", DOWN_AT.index((k, s))))
            if (k, s) in OUT_AT:
                kind, chunk, half = OUT_AT[k, s]
                if not (first and chunk == 1):
                    out.append((k, s, kind, (chunk, half)))
            if (k, s) in MAX_AT and not (last and k == SLOTS - 1):
                out.append((k, s, "max", MAX_AT[k, s]))
    return out


PRE_TILES = len(PROJ) + 2
FIRST_TILES = len(tiles_of(True, False))
MID_TILES = len(tiles_of(False, False))
assert PRE_TILES % 2 == 0 and FIRST_TILES % 2 == 0 and MID_TILES % 2 == 0


class Iteration:

    def __init__(self, i, first=False, last=False):
        self.i, self.first, self.last = i, first, last
        self.tiles = tiles_of(first, last)
        self.tile0 = PRE_TILES if first else PRE_TILES + FIRST_TILES + (i - 1) * MID_TILES

    def slot(self, k):
        return self.i * SLOTS + k

    def at(self, k, s):
        return [(n, t[2], t[3]) for n, t in enumerate(self.tiles) if t[:2] == (k, s)]

    def back(self, k, s, by):
        p = 4 * k + s - by
        return self.at(p // 4, p % 4) if p >= 0 else []


def build(nc, x_d, wq_d, wkv_d, wout_d, bout_d, u1_d, v1_d, b1_d, u2_d, v2_d, b2_d, rope_d, ident_d, out_d):
    with ExitStack() as ctx:
        def sb(name, shape, dt):
            return ctx.enter_context(nc.sbuf_tensor(name, shape, dt))

        def pb(name, shape, dt):
            return ctx.enter_context(nc.psum_tensor(name, shape, dt))

        def sem(name):
            return ctx.enter_context(nc.semaphore(name))

        X = sb("X", [P, TILES, D], F32)
        XT = sb("XT", [P, 2, B * N], F16)
        WQK = sb("WQK", [P, 2, 2, 2, HEADS * ROT], F16)
        WV = sb("WV", [P, 2, HEADS * DH], F16)
        WO = sb("WO", [P, HEADS * DH // P, D], F32)
        WOP = sb("WOP", [P, 2, HEADS * DH // P, D], F16)
        ROPE = sb("ROPE", [P, 2, N], F32)
        IDENT = sb("IDENT", [P, P], F32)
        IDENT16 = sb("IDENT16", [P, P], F16)
        BO = sb("BO", [P, D], F32)
        B2 = sb("B2", [P, D], F32)
        B1 = sb("B1", [P, FF // P], F32)
        B1R = sb("B1R", [FF // P, P], F32)
        U1 = sb("U1", [P, RANK], F32)
        V1 = sb("V1", [3 * RANK, FF], F32)
        U2 = sb("U2", [P, FF // P, RANK], F32)
        V2 = sb("V2", [4 * RANK, D], F32)
        U1P = sb("U1P", [P, 2, 3, RANK], F16)
        V1P = sb("V1P", [3 * RANK, FF], F16)
        U2P = sb("U2P", [P, FF // P, 2, RANK], F16)
        WRAW = sb("WRAW", [P, 3, HEADS * DH], F32)
        QK = sb("QK", [P, GH, 4, N], F16)
        KHH = QK[:, :, 0, :]
        KL1 = QK[:, :, 1, :]
        QHL = QK[:, :, 2, :]
        QHM = QK[:, :, 3, :]
        V = sb("V", [P, GH, KT * VP], F16)
        STAGE = sb("STAGE", [P, 4, 2, N], F16)
        KS, QS = STAGE[:, 0:2, :, :], STAGE[:, 2:4, :, :]
        VS = sb("VS", [P, GH, KT * VP], F16)
        T1 = sb("T1", [P, 512], F32)
        T2 = sb("T2", [P, 512], F32)
        YR = sb("YR", [P, 512], F32)
        PF = sb("PF", [P, 4, 1024], F32)
        PR = sb("PR", [P, 4, 1024], F16)
        OS = sb("OS", [P, 2, 2, VW], F32)
        ON = sb("ON", [P, 2, DH], F32)
        RS = sb("RS", [P, 2, 1], F32)
        MINUS_ONE = sb("MINUS_ONE", [P, 2, 1], F32)
        OG = sb("OG", [P, 2, KT, P], F32)
        OT = sb("OT", [P, 2, N], F16)
        MS = sb("MS", [P, 2, HALF // 2, N], F16)
        MN = sb("MN", [P, 2, KT], F16)
        ST = sb("ST", [P, TILES, 6], F32)
        MV = sb("MV", [P, TILES, 2], F32)
        VE = sb("VE", [P, TILES], F32)
        MINUS_HALF = sb("MINUS_HALF", [P, TILES], F32)
        RSTD = sb("RSTD", [P, TILES], F32)
        XN = PF[:, :, :].rearrange("p a (t d) -> p (a t) d", d=D)
        XN2 = WRAW[:, :, :].rearrange("p a (t d) -> p (a t) d", d=D)
        DOWN = STAGE[:, 0:2, :, :].rearrange("p a b c -> p (a b c)")
        H = [QK[:, h, :, :].rearrange("p a b -> p (a b)").bitcast(F32) for h in range(2)]
        HR = [QK[:, 2, 2 * a:2 * a + 2, :].rearrange("p a b -> p (a b)") for a in range(2)]
        QT = QK[:, 3, :, :].rearrange("p a b -> p (a b)").bitcast(F32)

        S = [pb(f"S{n}", [P, 2, QW], F32) for n in range(2)]
        M = [pb(f"M{n}", [P, 512], F32) for n in range(2)]
        O = [pb(f"O{n}", [P, 2, 256], F32) for n in range(2)]
        T = [pb(f"TILE{n}", [P, 512], F32) for n in range(2)]
        HB = [s[:, :, :].rearrange("p a b -> p (a b)") for s in S] + [m[:, :] for m in M]

        x_in = [sem(f"x_in{b}") for b in range(B)]
        w_in, wo_in, small_in, rope_in = sem("w_in"), sem("wo_in"), sem("small_in"), sem("rope_in")
        stats, aggr, var_eps, rstd, xn_made = (sem(n) for n in ("stats", "aggr", "var_eps", "rstd", "xn_made"))
        centred = sem("centred")
        xt_made, xt_hi, xt_lo = sem("xt_made"), sem("xt_hi"), sem("xt_lo")
        w_hi, w_lo, set_up, bias_in = sem("w_hi"), sem("w_lo"), sem("set_up"), sem("bias_in")
        tile_made = sem("tile_made")
        rot_read, rot_parts, rot_sum, rot_hi, rot_lo = (sem(f"rot_{n}") for n in ("read", "parts", "sum", "hi", "lo"))
        pass_hi, pass_lo, v_hi, v_lo = sem("pass_hi"), sem("pass_lo"), sem("v_hi"), sem("v_lo")
        turn_hi, turned, added = sem("turn_hi"), sem("turned"), sem("added")
        max_row = [sem(f"max_row{half}") for half in range(2)]
        wo_hi, wo_lo = sem("wo_hi"), sem("wo_lo")
        handed = [sem(f"handed{h}") for h in range(GH)]
        v_handed = [sem(f"v_handed{h}") for h in range(GH)]
        unit_made, unit_copied, folded, max_found = (sem(n) for n in ("unit_made", "unit_copied", "folded", "max_found"))
        scored, exped, rest_made = sem("scored"), sem("exped"), sem("rest_made")
        pv_done, o_copied, o_sum, normed = sem("pv_done"), sem("o_copied"), sem("o_sum"), sem("normed")
        f_w_hi, f_w_lo, f_xn = (sem(f"f_{n}") for n in ("w_hi", "w_lo", "xn"))
        f_xt_hi, f_xt_lo, f_down_hi, f_down_lo = (sem(f"f_{n}") for n in ("xt_hi", "xt_lo", "down_hi", "down_lo"))
        f_h, f_gelu, f_rest, f_q, f_qt, f_y, f_out, f_bias = (
            sem(f"f_{n}") for n in ("h", "gelu", "rest", "q", "qt", "y", "out", "bias"))
        stored = sem("stored")
        powers_set = sem("powers_set")
        b1_turned, b1_copied = sem("b1_turned"), sem("b1_copied")

        SMALL = 12 * 16

        def wait(e, s, value):
            if not (isinstance(value, int) and value <= 0):
                e.wait_ge(s, value)

        def freed(kind, args, it):
            if kind == "proj":
                w, c, t = args
                g = it.i + 1
                if t == "rot":
                    return rot_read, g * 4 + "qk".index(w) * 2 + c + 1
                if t == "pass":
                    return pass_lo, g * 4 + "qk".index(w) * 2 + c + 1
                return v_lo, g * 4 + c + 1
            if kind == "turn_x":
                return (xt_lo, f_xt_lo)[args[0]], args[1] + 1
            if kind == "down":
                return f_down_lo, args + 1
            if kind == "max":
                return max_row[args[1]], it.i * GH + 1 + args[0] + 1
            chunk, half = args
            nth = (it.i * 2 - chunk) * 2 + half + 1
            return (turned if kind == "turn" else added), nth

        def before(it, n):
            if n >= 2:
                return it.tiles[n - 2][2:], it
            if it.first:
                return [("proj", PROJ[-2 + n]), ("max", (-1, n))][1], it
            return Iteration(it.i - 1).tiles[n - 2][2:], Iteration(it.i - 1)

        def rows_of(nth):
            return (nth * KT, (nth + 1) * KT) if nth < B else ((nth - B) * CHUNK, (nth - B + 1) * CHUNK)

        def normalised(phase, t):
            if phase == 0:
                return XN[:, t, :] if t < KT else XN2[:, t - KT, :]
            return XN2[:, t, :] if t < EARLY * CHUNK else XN[:, t - EARLY * CHUNK, :]

        def ln_stats(e, nth):
            if nth < B:
                e.wait_ge(x_in[nth], 16)
            for t in range(*rows_of(nth)):
                bs = e.bn_stats(ST[:, t, :], X[:, t, :])
            bs.then_inc(stats, 1)

        def ln_aggr(e, nth):
            t0, t1 = rows_of(nth)
            e.wait_ge(stats, nth + 1)
            for t in range(t0, t1):
                ba = e.bn_aggr(MV[:, t, :], ST[:, t, :])
            ba.then_inc(aggr, 1)
            e.wait_ge(aggr, nth + 1)
            e.tensor_scalar(VE[:, t0:t1], MV[:, t0:t1, 1], EPS, None, ALU.add).then_inc(var_eps, 1)

        def ln_rstd(e, nth):
            t0, t1 = rows_of(nth)
            e.wait_ge(var_eps, nth + 1)
            e.tensor_tensor(RSTD[:, t0:t1], VE[:, t0:t1], MINUS_HALF[:, t0:t1], ALU.pow).then_inc(rstd, 1)

        def ln_apply(e, phase, c):
            e.wait_ge(rstd, (B + c if phase else c * CHUNK // KT) + 1)
            for t in range(CHUNK * c, CHUNK * c + CHUNK):
                ts = e.tensor_scalar(normalised(phase, t), X[:, t, :], MV[:, t, 0:1], RSTD[:, t:t + 1],
                                     ALU.subtract, ALU.mult)
            ts.then_inc((xn_made, f_xn)[phase], 1)

        def max_place(place, half):
            return QHM[DH:DH + 1, place, half * 512:(half + 1) * 512]

        def pool_apply(e, phase, c):
            e.wait_ge(rstd, (B + c if phase else c * CHUNK // KT) + 1)
            t0, at = CHUNK * c, CHUNK * c - (0 if phase else KT)
            nth = FC - PRE_CHUNKS + c if phase else c - PRE_CHUNKS
            xn = XN2[:, at:at + CHUNK, :]
            mean, scale = MV[:, t0:t0 + CHUNK, 0:1], RSTD[:, t0:t0 + CHUNK, None]
            e.tensor_tensor(xn, X[:, t0:t0 + CHUNK, :], mean.broadcast_to([P, CHUNK, D]),
                            ALU.subtract).then_inc(centred, 1)
            e.wait_ge(centred, nth + 1)
            e.tensor_tensor(xn, xn, scale.broadcast_to([P, CHUNK, D]), ALU.mult).then_inc((xn_made, f_xn)[phase], 1)

        def proj_tile(e, args, g, bank):
            w, c, t = args
            gi, b = g % GPB, g // GPB
            if w == "v":
                for r in range(2):
                    rows = bass.ds(b * N + (2 * c + r) * P, P)
                    cols = bass.ds(gi * GH * DH, GH * DH)
                    for n, (xp, wp) in enumerate(((0, 0), (0, 1), (1, 0))):
                        mm = e.matmul(T[bank][:, r * 256:(r + 1) * 256], XT[:, xp, rows], WV[:, wp, cols],
                                      start=(n == 0), stop=(n == 2))
            else:
                rows, cols = bass.ds(b * N + c * 512, 512), bass.ds(gi * GH * ROT, GH * ROT)
                kind = ("rot", "pass").index(t)
                for n, (xp, wp) in enumerate(((0, 0), (0, 1), (1, 0))):
                    mm = e.matmul(T[bank][:, :], WQK[:, "qk".index(w), wp, kind, cols], XT[:, xp, rows],
                                  start=(n == 0), stop=(n == 2))
            mm.then_inc(tile_made, 1)

        def max_tile(e, head, side, half, bank):
            if half == 0:
                e.wait_ge(max_found, 2 * head + 2)
            for j in range(4):
                mm = e.matmul(T[bank][DH:DH + 1, j * P:(j + 1) * P], MN[:, side, half * 4 + j:half * 4 + j + 1],
                              IDENT16[:, :], start=True, stop=True)
            mm.then_inc(tile_made, 1)

        def turn_tile(e, chunk, half, bank):
            for j in range(4):
                mm = e.transpose(T[bank][:, j * P:(j + 1) * P], OG[:, chunk, half * 4 + j, :], IDENT[:, :])
            mm.then_inc(tile_made, 1)

        def out_tile(e, chunk, half, bank, pair):
            for j in range(4):
                q = half * 4 + j
                for n, (op, wp) in enumerate(((0, 0), (0, 1), (1, 0))):
                    mm = e.matmul(T[bank][:, j * P:(j + 1) * P], OT[:, op, q * P:(q + 1) * P], WOP[:, wp, pair, :],
                                  start=(n == 0), stop=(n == 2))
            mm.then_inc(tile_made, 1)

        def turn_x_tile(e, phase, c, bank):
            e.wait_ge((xn_made, f_xn)[phase], c + 1)
            for j in range(CHUNK):
                mm = e.transpose(T[bank][:, j * P:(j + 1) * P], normalised(phase, CHUNK * c + j), IDENT[:, :])
            mm.then_inc(tile_made, 1)

        def down_tile(e, c, bank):
            if c == 0:
                e.wait_ge(f_w_lo, 5)
            e.wait_ge(f_xt_lo, c + 1)
            rows = slice(c * 512, (c + 1) * 512)
            for n, (wp, xp) in enumerate(((0, 0), (1, 0), (0, 1))):
                mm = e.matmul(T[bank][0:3 * RANK, :], U1P[:, wp, :, :].rearrange("p a r -> p (a r)"),
                              XT[:, xp, rows], start=(n == 0), stop=(n == 2))
            mm.then_inc(tile_made, 1)

        def pe_tiles(e, it, k, s):
            for n, kind, args in it.at(k, s):
                (kind0, args0), it0 = before(it, n)
                e.wait_ge(*freed(kind0, args0, it0))
                bank = n % 2
                if kind == "proj":
                    proj_tile(e, args, it.i + 1, bank)
                elif kind == "max":
                    max_tile(e, it.i * GH + 1 + args[0], (1 + args[0]) % 2, args[1], bank)
                elif kind == "turn_x":
                    turn_x_tile(e, *args, bank)
                elif kind == "down":
                    down_tile(e, args, bank)
                elif kind == "turn":
                    chunk, half = args
                    e.wait_ge(normed, it.slot(8 if chunk == 0 else 0))
                    turn_tile(e, chunk, half, bank)
                else:
                    chunk, half = args
                    e.wait_ge(*freed("turn", (chunk, 1), it))
                    out_tile(e, chunk, half, bank, ((it.i - chunk) % GPB) * 2 + chunk)

        def pe_scores(e, it, k, s):
            n, h, quarter = it.slot(k), k // 4, k % 4
            if quarter % 2 == 0 and s == 0:
                e.wait_ge(max_row[quarter // 2], it.i * GH + h + 1)
            wait(e, exped, 4 * n + s - 1)
            for kk in range(2):
                keys = slice((2 * s + kk) * P, (2 * s + kk + 1) * P)
                rows = slice(quarter * QW, (quarter + 1) * QW)
                e.matmul(S[s % 2][:, kk, :], KHH[:, h, keys], QHL[:, h, rows], start=True, stop=False)
                mm = e.matmul(S[s % 2][:, kk, :], KL1[0:DH + 1, h, keys], QHM[0:DH + 1, h, rows],
                              start=False, stop=True)
            mm.then_inc(scored, 1)

        def pe_values(e, n, k, s, fills):
            qt, half, h, bank = s % 2, s // 2, (k % SLOTS) // 4, k % 2
            if s == 0:
                wait(e, o_copied, n - 1)
                if k % 4 == 0:
                    e.wait_ge(v_handed[h], 16 * (fills + 1))
            if qt == 0:
                e.wait_ge(rest_made, 2 * n + half + 1)
            buf = (2 * k + half) % 4
            hi = PF[:, buf, :].bitcast(BF16)
            for j in range(4):
                kt = half * 4 + j
                at = j * QW + qt * P
                vals = V[:, h, kt * VP:kt * VP + VW]
                e.matmul(O[bank][:, qt, 0:VW], hi[:, 2 * at + 1:2 * (at + P):2], vals,
                         start=(s == 0 and j == 0), stop=False, skip_group_check=True)
                mm = e.matmul(O[bank][:, qt, 0:VW], PR[:, buf, at:at + P], vals,
                              start=False, stop=(half == 1 and j == 3), skip_group_check=True)
            if qt == 1:
                mm.then_inc(pv_done, 1)

        def pe_slot(e, it, k):
            for s in range(4):
                back = 4 * k + s - PV_LAG
                if not it.first or back >= 0:
                    pe_values(e, it.slot(back // 4), back // 4, back % 4, it.i)
                pe_tiles(e, it, k, s)
                pe_scores(e, it, k, s)
                if not (it.last and 4 * k + LEAD + s >= GH * UNITS):
                    place_u = 4 * k + LEAD + s
                    fills = it.i + place_u // (GH * UNITS) + 1
                    u = it.slot(k) * 4 + LEAD + s
                    place, unit = (place_u // UNITS) % GH, place_u % UNITS
                    if unit == 0:
                        e.wait_ge(handed[place], HAND * fills)
                    e.wait_ge(unit_copied, u - 1)
                    e.matmul(M[s % 2][:, :], QHL[:, place, (unit // 2) * P:(unit // 2 + 1) * P],
                             KHH[:, place, (unit % 2) * 512:(unit % 2 + 1) * 512],
                             start=True, stop=True).then_inc(unit_made, 1)

        def act_tile(e, kind, args, made, g, bank):
            if kind == "proj" and args[2] == "pass":
                w, c, _ = args
                st = (QS, KS)["qk".index(w)]
                e.wait_ge(tile_made, made)
                if w == "q" and c == 0:
                    for h in range(GH):
                        wait(e, handed[h], HAND * g)
                e.activation(st[:, 0, 1, c * 512:(c + 1) * 512], T[bank][:, :], ACT.Copy).then_inc(pass_hi, 1)
            elif kind == "proj" and args[2] == "v":
                c = args[1]
                e.wait_ge(tile_made, made)
                if c == 0:
                    for h in range(GH):
                        wait(e, v_handed[h], 16 * g)
                for r in range(2):
                    dst = VS[:, :, :].rearrange("p h (t v) -> p h t v", v=VP)[:, :, 2 * c + r, 0:DH]
                    src = T[bank][:, r * 256:(r + 1) * 256].rearrange("p (h d) -> p h d", d=DH)
                    cp = e.activation(dst, src, ACT.Copy)
                cp.then_inc(v_hi, 1)

        def act_rot(e, args, g):
            w, c, _ = args
            st, nth = (QS, KS)["qk".index(w)], "qk".index(w) * 2 + c
            e.wait_ge(rot_sum, g * 4 + nth + 1)
            if nth == 0:
                for h in range(GH):
                    wait(e, handed[h], HAND * g)
            e.activation(st[:, 0, 0, c * 512:(c + 1) * 512], YR[:, :], ACT.Copy).then_inc(rot_hi, 1)

        def act_turn_x(e, phase, c, made, bank):
            e.wait_ge(tile_made, made)
            e.activation(XT[:, 0, c * 512:(c + 1) * 512], T[bank][:, :],
                         ACT.Copy).then_inc((xt_hi, f_xt_hi)[phase], 1)

        def act_down(e, c, made, bank):
            e.wait_ge(tile_made, made)
            if c == 0:
                for h in range(GH):
                    e.wait_ge(handed[h], HAND * GROUPS)
            e.activation(DOWN[0:3 * RANK, c * 512:(c + 1) * 512], T[bank][0:3 * RANK, :],
                         ACT.Copy).then_inc(f_down_hi, 1)

        def act_tiles(e, it, k, s):
            for n, kind, args in it.at(k, s):
                made, bank = it.tile0 + n + 1, n % 2
                if kind == "proj":
                    act_tile(e, kind, args, made, it.i + 1, bank)
                elif kind == "max" and args[1] == 1:
                    wait(e, scored, (it.i * GH + 1 + args[0]) * 16 - 48)
                    e.wait_ge(tile_made, made)
                    e.activation(max_place((1 + args[0]) % GH, 1), T[bank][DH:DH + 1, :],
                                 ACT.Copy).then_inc(max_row[1], 1)
                elif kind == "turn_x":
                    act_turn_x(e, *args, made, bank)
                elif kind == "down":
                    act_down(e, args, made, bank)
                elif kind == "turn":
                    e.wait_ge(tile_made, made)
                    e.activation(OT[:, 0, args[1] * 512:(args[1] + 1) * 512], T[bank][:, :],
                                 ACT.Copy).then_inc(turn_hi, 1)
            for n, kind, args in it.back(k, s, 4):
                if kind == "proj" and args[2] == "rot":
                    act_rot(e, args, it.i + 1)

        def act_copy_out(e, n, k):
            e.wait_ge(pv_done, 2 * n + 2)
            wait(e, normed, n - 1)
            e.activation(OS[:, k % 2, :, :], O[k % 2][:, :, 0:VW], ACT.Copy).then_inc(o_copied, 1)

        def act_unit(e, u, half, place_u, bank):
            e.wait_ge(unit_made, u + 1)
            if place_u % HALF == 0:
                wait(e, max_found, half - 1)
            q, c = (place_u % HALF) // 2, place_u % 2
            e.activation(MS[:, (place_u // HALF) % 2, q, c * 512:(c + 1) * 512], bank, ACT.Copy,
                         scale=-1.0 / MSCALE).then_inc(unit_copied, 1)

        def act_slot(e, it, k):
            n = it.slot(k)
            for s in range(4):
                place_u = 4 * k + s + LEAD - 1
                if not (it.last and place_u >= GH * UNITS):
                    act_unit(e, 4 * n + s + LEAD - 1, it.i * (GH * UNITS // HALF) + place_u // HALF, place_u,
                             M[place_u % 2][:, :])
                if s == 1 and (not it.first or k >= 2):
                    act_copy_out(e, it.slot(k - 2), k)
                act_tiles(e, it, k, s)
                e.wait_ge(scored, 4 * n + s + 1)
                if s % 2 == 0:
                    wait(e, pv_done, 2 * n - 3 + s // 2)
                e.activation(PF[:, (2 * k + s // 2) % 4, (s % 2) * 512:(s % 2 + 1) * 512],
                             S[s % 2][:, :, :].rearrange("p a b -> p (a b)"), ACT.Exp,
                             scale=EXP_SCALE).then_inc(exped, 1)

        def dve_tile(e, kind, args, made, g, bank):
            w, c, t = args
            nth = "qkv".index(w) * 2 + c
            cols = slice(c * 512, (c + 1) * 512)
            if t == "rot":
                e.wait_ge(tile_made, made)
                wait(e, rot_sum, g * 4 + nth)
                e.tensor_tensor(T1[:, :], T[bank][:, :], ROPE[:, 0, cols], ALU.mult)
                e.stream_shuffle(T2[:, :], T[bank][:, :], [lane ^ 1 for lane in range(32)]).then_inc(rot_read, 1)
            elif t == "pass":
                st = (QS, KS)["qk".index(w)]
                e.wait_ge(pass_hi, g * 4 + nth + 1)
                e.tensor_tensor(st[:, 1, 1, cols], T[bank][:, :], st[:, 0, 1, cols], ALU.subtract).then_inc(pass_lo, 1)
            else:
                e.wait_ge(v_hi, g * 4 + c + 1)
                vs = VS[:, :, :].rearrange("p h (t v) -> p h t v", v=VP)
                for r in range(2):
                    src = T[bank][:, r * 256:(r + 1) * 256].rearrange("p (h d) -> p h d", d=DH)
                    tt = e.tensor_tensor(vs[:, :, 2 * c + r, DH:2 * DH], src, vs[:, :, 2 * c + r, 0:DH], ALU.subtract)
                tt.then_inc(v_lo, 1)

        def dve_turn(e, half, nth, bank):
            cols = slice(half * 512, (half + 1) * 512)
            e.wait_ge(turn_hi, nth)
            e.tensor_tensor(OT[:, 1, cols], T[bank][:, :], OT[:, 0, cols], ALU.subtract).then_inc(turned, 1)

        def dve_add(e, xs, bank):
            e.scalar_tensor_tensor(xs, T[bank][:, :].rearrange("p (t d) -> p t d", d=D), 1.0 / WSCALE, xs,
                                   ALU.mult, ALU.add).then_inc(added, 1)

        def dve_tiles(e, it, k, s):
            for n, kind, args in it.back(k, s, 1):
                made, bank = it.tile0 + n + 1, n % 2
                if kind == "proj":
                    dve_tile(e, kind, args, made, it.i + 1, bank)
                elif kind == "turn_x":
                    dve_turn_x(e, *args, bank)
                elif kind == "down":
                    dve_down(e, args, bank)
                elif kind == "out":
                    chunk, half = args
                    b = (it.i - chunk) // GPB
                    e.wait_ge(tile_made, made)
                    xs = X[:, bass.ds(b * KT + half * 4, 4), :]
                    dve_add(e, xs, bank)
                elif kind == "max" and args[1] == 0:
                    wait(e, scored, (it.i * GH + 1 + args[0]) * 16 - 48)
                    e.wait_ge(tile_made, made)
                    e.tensor_copy(max_place((1 + args[0]) % GH, 0), T[bank][DH:DH + 1, :]).then_inc(max_row[0], 1)
                elif kind == "turn":
                    dve_turn(e, args[1], freed(kind, args, it)[1], bank)

        def dve_turn_x(e, phase, c, bank):
            cols = slice(c * 512, (c + 1) * 512)
            e.wait_ge((xt_hi, f_xt_hi)[phase], c + 1)
            e.tensor_tensor(XT[:, 1, cols], T[bank][:, :], XT[:, 0, cols],
                            ALU.subtract).then_inc((xt_lo, f_xt_lo)[phase], 1)

        def dve_down(e, c, bank):
            mid = DOWN[RANK:2 * RANK, c * 512:(c + 1) * 512]
            e.wait_ge(f_down_hi, c + 1)
            e.tensor_tensor(mid, T[bank][RANK:2 * RANK, :], mid, ALU.subtract).then_inc(f_down_lo, 1)

        def dve_first(e, k, s):
            if s == 1 and k in STATS_AT:
                ln_stats(e, STATS_AT[k])
            if s == 3 and k in STATS_AT:
                ln_aggr(e, STATS_AT[k])

        def dve_last(e, k, s):
            if s == 1 and k < EARLY:
                ln_stats(e, B + k)
            if s == 3 and k < EARLY:
                ln_aggr(e, B + k)

        def split_out_weights(e):
            e.wait_ge(wo_in, 16)
            e.tensor_scalar(WOP[:, 0, :, :], WO[:, :, :], WSCALE, None, ALU.mult).then_inc(wo_hi, 1)
            e.wait_ge(wo_hi, 1)
            e.scalar_tensor_tensor(WOP[:, 1, :, :], WO[:, :, :], WSCALE, WOP[:, 0, :, :], ALU.mult,
                                   ALU.subtract).then_inc(wo_lo, 1)

        def split_ff_weights(e):
            e.wait_ge(small_in, SMALL)
            for r in range(3):
                e.tensor_scalar(U1P[:, 0, r, :], U1[:, :], WSCALE, None, ALU.mult).then_inc(f_w_hi, 1)
            e.tensor_scalar(V1P[:, :], V1[:, :], WSCALE, None, ALU.mult).then_inc(f_w_hi, 1)
            e.tensor_scalar(U2P[:, :, 0, :], U2[:, :, :], WSCALE, None, ALU.mult).then_inc(f_w_hi, 1)
            e.wait_ge(f_w_hi, 5)
            for r in range(3):
                e.scalar_tensor_tensor(U1P[:, 1, r, :], U1[:, :], WSCALE, U1P[:, 0, r, :], ALU.mult,
                                       ALU.subtract).then_inc(f_w_lo, 1)
            low = V1P[2 * RANK:3 * RANK, :]
            e.scalar_tensor_tensor(low, V1[2 * RANK:3 * RANK, :], WSCALE, low, ALU.mult,
                                   ALU.subtract).then_inc(f_w_lo, 1)
            e.scalar_tensor_tensor(U2P[:, :, 1, :], U2[:, :, :], WSCALE, U2P[:, :, 0, :], ALU.mult,
                                   ALU.subtract).then_inc(f_w_lo, 1)

        def dve_fold(e, half, place, part):
            ms = MS[:, place % 2, :, :]
            if part == 0:
                e.wait_ge(unit_copied, (half + 1) * HALF)
            for level in ((0,), (1, 2), (3,))[part]:
                w = N // 2 >> level
                if level:
                    e.wait_ge(folded, half * FOLDS + level)
                e.tensor_tensor(ms[:, :, 0:w], ms[:, :, 0:w], ms[:, :, w:2 * w], ALU.min).then_inc(folded, 1)
            if part == 2:
                e.wait_ge(folded, (half + 1) * FOLDS)
                e.tensor_reduce(MN[:, (place // 2) % 2, (place % 2) * 4:(place % 2) * 4 + 4], ms[:, :, 0:w], AX,
                                ALU.min).then_inc(max_found, 1)

        def dve_rest(e, n, k, pair):
            buf = (2 * k + pair) % 4
            e.wait_ge(exped, 4 * n + 2 * pair + 2)
            e.tensor_tensor(PR[:, buf, :], PF[:, buf, :], PF[:, buf, :].bitcast(BF16)[:, 1:2048:2],
                            ALU.subtract).then_inc(rest_made, 1)

        def dve_slot(e, it, k):
            n = it.slot(k)
            for s in range(4):
                dve_tiles(e, it, k, s)
                if it.first:
                    dve_first(e, k, s)
                if it.last:
                    dve_last(e, k, s)
                if s == 0 and (not it.first or k > 0):
                    dve_rest(e, it.slot(k - 1), k - 1, 1)
                if s == 2:
                    dve_rest(e, n, k, 0)
                for part in range(3):
                    place_u = 4 * k + s + LEAD - 2 - part
                    if place_u % HALF == HALF - 1 and not (it.last and place_u >= GH * UNITS):
                        place = place_u // HALF
                        dve_fold(e, it.i * (GH * UNITS // HALF) + place, place, part)

        def rot_add(e, args, g):
            w, c, _ = args
            nth = g * 4 + "qk".index(w) * 2 + c
            e.wait_ge(rot_read, nth + 1)
            e.tensor_tensor(T2[:, :], T2[:, :], ROPE[:, 1, c * 512:(c + 1) * 512], ALU.mult).then_inc(rot_parts, 1)
            e.wait_ge(rot_parts, nth + 1)
            wait(e, rot_lo, nth)
            e.tensor_tensor(YR[:, :], T1[:, :], T2[:, :], ALU.add).then_inc(rot_sum, 1)

        def rot_low(e, args, g):
            w, c, _ = args
            st, nth = (QS, KS)["qk".index(w)], "qk".index(w) * 2 + c
            cols = slice(c * 512, (c + 1) * 512)
            e.wait_ge(rot_hi, g * 4 + nth + 1)
            e.tensor_tensor(st[:, 1, 0, cols], YR[:, :], st[:, 0, 0, cols], ALU.subtract).then_inc(rot_lo, 1)

        def pool_norm(e, n, k):
            h, side, q = (k % SLOTS) // 4, k % 2, (k % 4) * 2
            e.wait_ge(o_copied, n + 1)
            wait(e, normed, n)
            e.tensor_tensor(ON[:, :, :], OS[:, side, :, 0:DH], OS[:, side, :, DH:2 * DH], ALU.add).then_inc(o_sum, 1)
            e.tensor_tensor(RS[:, :, :], OS[:, side, :, 2 * DH:VW], MINUS_ONE[:, :, :], ALU.pow).then_inc(o_sum, 1)
            e.wait_ge(o_sum, 2 * n + 2)
            e.tensor_tensor(OG[:, h // 2, q:q + 2, (h % 2) * DH:(h % 2 + 1) * DH], ON[:, :, :],
                            RS[:, :, :].broadcast_to([P, 2, DH]), ALU.mult).then_inc(normed, 1)

        def pool_bias(e, phase, c):
            e.wait_ge((xn_made, f_xn)[phase], c + 1)
            xs = X[:, CHUNK * c:CHUNK * c + CHUNK, :]
            e.tensor_tensor(xs, xs, (BO, B2)[phase][:, None, :].broadcast_to([P, CHUNK, D]),
                            ALU.add).then_inc((bias_in, f_bias)[phase], 1)

        def pool_slot(e, it, k):
            for s in range(4):
                for n, kind, args in it.back(k, s, 5):
                    if kind == "proj" and args[2] == "rot":
                        rot_low(e, args, it.i + 1)
                for n, kind, args in it.back(k, s, 1):
                    if kind == "proj" and args[2] == "rot":
                        rot_add(e, args, it.i + 1)
                if s == 2 and (not it.first or k >= 2):
                    if k - 2 == 0 and not it.first:
                        e.wait_ge(*freed("turn", (0, 1), Iteration(it.i - 1)))
                    if k - 2 == 8 and not it.first:
                        e.wait_ge(*freed("turn", (1, 1), it))
                    pool_norm(e, it.slot(k - 2), k - 2)
                if it.first and s == 0 and k - 1 in STATS_AT:
                    ln_rstd(e, STATS_AT[k - 1])
                if (k, s) in APPLY_AT and it.first:
                    pool_apply(e, 0, PRE_CHUNKS + APPLY_AT.index((k, s)))
                if it.first and (k, s) in BIAS_AT:
                    pool_bias(e, 0, PRE_CHUNKS + BIAS_AT.index((k, s)))
                if it.last and s == 0 and 1 <= k <= EARLY:
                    ln_rstd(e, B + k - 1)
                    pool_apply(e, 1, k - 1)
                if it.last and s == 0 and 2 <= k <= EARLY + 1:
                    pool_bias(e, 1, k - 2)

        def hand_over(sp, what, h):
            rows = slice(32 * h, 32 * h + 32)
            if what == "v":
                sp.dma_start(V[:, h, :], VS[:, h, :]).then_inc(v_handed[h], 16)
                return
            for t in range(2):
                top, low = slice(32 * t, 32 * t + 32), slice(DH + 32 * t, DH + 32 * t + 32)
                sp.dma_start(QK[top, h, 0:2, :], STAGE[rows, 0:2, t, :]).then_inc(handed[h], 16)
                sp.dma_start(QK[top, h, 2:4, :], STAGE[rows, 2:3, t, :].broadcast_to([32, 2, N])).then_inc(handed[h], 16)
                sp.dma_start(QK[low, h, 0:3:2, :], STAGE[rows, 0:4:3, t, :]).then_inc(handed[h], 16)

        def sp_iteration(sp, it):
            for what, h in HAND_ORDER:
                if (it.first if h == GH - 1 else it.last):
                    continue
                if what == "v":
                    if h == 0:
                        sp.wait_ge(v_lo, (it.i + 1) * 4 + 4)
                    sp.wait_ge(pv_done, ((it.i - (h == GH - 1)) * 16 + 4 * h + 4) * 2)
                elif h == 0:
                    sp.wait_ge(rot_lo, (it.i + 1) * 4 + 4)
                    sp.wait_ge(pass_lo, (it.i + 1) * 4 + 4)
                else:
                    sp.wait_ge(scored, (it.i - (h == GH - 1)) * 64 + 16 * h + 16)
                hand_over(sp, what, h)

        block = ctx.enter_context(nc.Block())

        def loop(e, body):
            body(e, Iteration(0, first=True))
            with e.Fori(1, GROUPS - 1) as i:
                body(e, Iteration(i))
            body(e, Iteration(GROUPS - 1, last=True))

        END = GROUPS * SLOTS
        tail0 = PRE_TILES + FIRST_TILES + (GROUPS - 2) * MID_TILES + len(tiles_of(False, True))
        assert tail0 % 2 == 0

        @block.sync
        def _(sp):
            xr = x_d.rearrange("b (t p) d -> p (b t) d", p=P)
            sp.dma_start(X[:, 0:KT, :], xr[:, 0:KT, :]).then_inc(x_in[0], 16)
            sp.dma_start(IDENT[:, :], ident_d).then_inc(rope_in, 16)
            sp.dma_start(WRAW[:, 1:3, :], wkv_d.rearrange("p (a n) -> p a n", a=2)).then_inc(w_in, 16)
            sp.dma_start(ROPE[:, :, :], rope_d.rearrange("p (a n) -> p a n", a=2)).then_inc(rope_in, 16)
            for b in range(1, B):
                sp.dma_start(X[:, b * KT:(b + 1) * KT, :], xr[:, b * KT:(b + 1) * KT, :]).then_inc(x_in[b], 16)
            sp.dma_start(WO[:, :, :], wout_d.rearrange("(c p) n -> p c n", p=P)).then_inc(wo_in, 16)
            sp.wait_ge(rot_lo, 4)
            sp.wait_ge(pass_lo, 4)
            sp.wait_ge(set_up, 3)
            for h in range(GH):
                hand_over(sp, "qk", h)
            sp.wait_ge(v_lo, 4)
            for h in range(GH):
                hand_over(sp, "v", h)
            loop(sp, sp_iteration)
            for c in range(FC):
                sp.wait_ge(f_out, c + 1)
                sp.dma_start(out_d.rearrange("b (t p) d -> p (b t) d", p=P)[:, 4 * c:4 * c + 4, :],
                             X[:, 4 * c:4 * c + 4, :]).then_inc(stored, 16)
            sp.wait_ge(stored, 16 * FC)

        @block.gpsimd
        def _(pool):
            pool.memset(MINUS_HALF[:, :], -0.5).then_inc(powers_set, 1)
            pool.memset(MINUS_ONE[:, :, :], -1.0).then_inc(powers_set, 1)
            pool.wait_ge(powers_set, 2)
            pool.memset(QK[DH:DH + 32, :, 1, :], MSCALE).then_inc(set_up, 1)
            pool.wait_ge(set_up, 1)
            pool.memset(VS[:, :, :].rearrange("p h (t v) -> p h t v", v=VP)[:, :, :, 2 * DH:VP], WSCALE).then_inc(set_up, 1)
            pool.wait_ge(set_up, 2)
            ln_rstd(pool, 0)
            pool.wait_ge(rope_in, 32)
            pool.tensor_copy(IDENT16[:, :], IDENT[:, :]).then_inc(set_up, 1)
            for args in PROJ:
                if args[2] == "rot":
                    rot_low(pool, args, 0)
            ln_rstd(pool, 1)
            pool.wait_ge(small_in, SMALL)
            for c in range(PRE_CHUNKS):
                pool_bias(pool, 0, c)

            def body(e, it):
                for k in range(SLOTS):
                    pool_slot(e, it, k)

            loop(pool, body)
            pool_norm(pool, END - 2, SLOTS - 2)
            pool_norm(pool, END - 1, SLOTS - 1)
            for c in range(EARLY, FC):
                ln_rstd(pool, B + c)
            for c in range(EARLY, FC):
                pool_bias(pool, 1, c)

        @block.scalar
        def _(act):
            act.dma_start(WRAW[:, 0, :], wq_d).then_inc(w_in, 16)
            act.dma_start(BO[:, :], bout_d.rearrange("(a n) -> a n", a=1).broadcast_to([P, D])).then_inc(small_in, 16)
            act.dma_start(B2[:, :], b2_d.rearrange("(a n) -> a n", a=1).broadcast_to([P, D])).then_inc(small_in, 16)
            act.dma_start(B1R[:, :], b1_d.rearrange("(c p) -> c p", p=P)).then_inc(small_in, 16)
            act.dma_start(U1[:, :], u1_d).then_inc(small_in, 16)
            for r in range(3):
                act.dma_start(V1[r * RANK:(r + 1) * RANK, :], v1_d).then_inc(small_in, 16)
            act.dma_start(U2[:, :, :], u2_d.rearrange("(c p) r -> p c r", p=P)).then_inc(small_in, 16)
            for r in range(4):
                act.dma_start(V2[r * RANK:(r + 1) * RANK, :], v2_d).then_inc(small_in, 16)

            def w_part(w):
                if w < 2:
                    src = WRAW[:, w, :].rearrange("p (h d) -> p h d", d=DH)
                    for kind, d0 in ((0, 0), (1, ROT)):
                        act.activation(WQK[:, w, 0, kind, :].rearrange("p (h d) -> p h d", d=ROT),
                                       src[:, :, d0:d0 + ROT], ACT.Copy, scale=WSCALE).then_inc(w_hi, 1)
                else:
                    act.activation(WV[:, 0, :], WRAW[:, 2, :], ACT.Copy, scale=WSCALE).then_inc(w_hi, 1)

            def xt_part(c):
                act.wait_ge(xt_made, c + 1)
                act.activation(XT[:, 0, c * 512:(c + 1) * 512], S[c % 2][:, :, :].rearrange("p a b -> p (a b)"),
                               ACT.Copy).then_inc(xt_hi, 1)

            act.wait_ge(w_in, 32)
            for w in range(3):
                w_part(w)
            xt_part(0)
            xt_part(1)
            for n, args in enumerate(PROJ):
                act_tile(act, "proj", args, n + 1, 0, n % 2)
                if args[2] == "pass":
                    act_rot(act, args, 0)
            act.wait_ge(b1_turned, 1)
            act.activation(B1[:, :], M[0][:, 0:FF // P], ACT.Copy).then_inc(b1_copied, 1)
            for u in range(LEAD - 1):
                act_unit(act, u, u // HALF, u, HB[u % 4])
                if u == UNITS + 2:
                    act.wait_ge(tile_made, PRE_TILES)
                    act.activation(max_place(0, 1), T[1][DH:DH + 1, :], ACT.Copy).then_inc(max_row[1], 1)

            def body(e, it):
                for k in range(SLOTS):
                    act_slot(e, it, k)

            loop(act, body)
            act_copy_out(act, END - 2, SLOTS - 2)
            act_copy_out(act, END - 1, SLOTS - 1)
            def gelu(c):
                wait(act, f_q, c - 1)
                for f in range(FF // P):
                    act.wait_ge(f_h, 4 * c + f + 1)
                    act.activation(H[c % 2][:, f * 512:(f + 1) * 512], HB[f], ACT.Gelu_apprx_tanh,
                                   bias=B1[:, f:f + 1], scale=1.0 / (WSCALE * WSCALE)).then_inc(f_gelu, 1)

            def q_copy(c):
                act.wait_ge(f_q, c + 1)
                wait(act, f_y, c - 3)
                act.activation(QT[:, (c % 4) * 512:(c % 4 + 1) * 512],
                               O[c % 2][:, :, :].rearrange("p a b -> p (a b)"), ACT.Copy,
                               scale=1.0 / WSCALE).then_inc(f_qt, 1)

            gelu(0)
            for half in range(2):
                act.wait_ge(tile_made, tail0 + half + 1)
                act.activation(OT[:, 0, half * 512:(half + 1) * 512], T[half][:, :], ACT.Copy).then_inc(turn_hi, 1)
            for c in range(FC):
                if c + 1 < FC:
                    gelu(c + 1)
                q_copy(c)
                for late in range(EARLY, FC):
                    if c == 2:
                        act_turn_x(act, 1, late, tail0 + 4 + late - EARLY + 1, late % 2)
                    if c == 3:
                        act_down(act, late, tail0 + 6 + late - EARLY + 1, late % 2)

        @block.tensor
        def _(pe):
            pe.wait_ge(rope_in, 32)
            for c in range(PRE_CHUNKS):
                pe.wait_ge(xn_made, c + 1)
                for j in range(CHUNK):
                    mm = pe.transpose(HB[c][:, j * P:(j + 1) * P], normalised(0, c * CHUNK + j), IDENT[:, :])
                mm.then_inc(xt_made, 1)
            pe.wait_ge(xt_lo, 2)
            pre = Iteration(-1)
            for n, args in enumerate(PROJ):
                w, c, t = args
                if w == "v":
                    pe.wait_ge(w_lo, 5)
                else:
                    pe.wait_ge(w_lo, 2 * "qk".index(w) + (t == "pass") + 1)
                if n >= 2:
                    pe.wait_ge(*freed("proj", PROJ[n - 2], pre))
                proj_tile(pe, args, 0, n % 2)
            pe.wait_ge(small_in, SMALL)
            pe.transpose(M[0][:, 0:FF // P], B1R[:, :], IDENT[0:FF // P, 0:FF // P]).then_inc(b1_turned, 1)
            pe.wait_ge(b1_copied, 1)
            pe.wait_ge(set_up, 3)
            for u in range(LEAD):
                if u % UNITS == 0:
                    pe.wait_ge(handed[u // UNITS], HAND)
                wait(pe, unit_copied, u - 3)
                unit = u % UNITS
                pe.matmul(HB[u % 4], QHL[:, u // UNITS, (unit // 2) * P:(unit // 2 + 1) * P],
                          KHH[:, u // UNITS, (unit % 2) * 512:(unit % 2 + 1) * 512],
                          start=True, stop=True).then_inc(unit_made, 1)
                if u == UNITS + 2:
                    for half in range(2):
                        pe.wait_ge(*freed("proj", PROJ[len(PROJ) - 2 + half], pre))
                        max_tile(pe, 0, 0, half, half)
            pe.wait_ge(unit_copied, LEAD - 2)

            def body(e, it):
                for k in range(SLOTS):
                    if k == 12 and it.first:
                        e.wait_ge(wo_lo, 1)
                    pe_slot(e, it, k)

            loop(pe, body)
            for back in range(4 * SLOTS - PV_LAG, 4 * SLOTS):
                pe_values(pe, END - SLOTS + back // 4, back // 4, back % 4, GROUPS - 1)
            def up(c):
                pe.wait_ge(f_down_lo, c + 1)
                for f in range(FF // P):
                    wait(pe, f_gelu, 4 * (c - 1) + f + 1)
                    pe.matmul(HB[f], V1P[:, f * P:(f + 1) * P], DOWN[0:3 * RANK, c * 512:(c + 1) * 512],
                              start=True, stop=True).then_inc(f_h, 1)

            def down2(c):
                wait(pe, f_qt, c - 1)
                for f in range(FF // P):
                    pe.wait_ge(f_gelu, 4 * c + f + 1)
                    pe.wait_ge(f_rest, 2 * c + f // 2 + 1)
                    upper = H[c % 2][:, :].bitcast(BF16)[:, f * 1024 + 1:(f + 1) * 1024:2]
                    for part, h in enumerate((upper, HR[c % 2][:, f * 512:(f + 1) * 512])):
                        mm = pe.matmul(O[c % 2][part * 2 * RANK:(part + 1) * 2 * RANK, :, :].rearrange("p a b -> p (a b)"),
                                       U2P[:, f, :, :].rearrange("p a r -> p (a r)"), h,
                                       start=(f == 0), stop=(f == FF // P - 1))
                mm.then_inc(f_q, 1)

            def up2(c):
                pe.wait_ge(f_qt, c + 1)
                if c < 2:
                    pe.wait_ge(added, GROUPS * 4)
                elif c < 4:
                    pe.wait_ge(f_down_lo, EARLY + c - 2 + 1)
                else:
                    pe.wait_ge(f_out, c - 1)
                for j in range(CHUNK):
                    at = (c % 4) * 512 + j * P
                    mm = pe.matmul(T[c % 2][:, j * P:(j + 1) * P], QT[:, at:at + P], V2[:, :],
                                   start=True, stop=True)
                mm.then_inc(f_y, 1)

            pe.wait_ge(unit_copied, 64 * UNITS)
            pe.wait_ge(exped, 4 * END)
            up(0)
            pe.wait_ge(normed, END)
            lastit = Iteration(GROUPS - 1, last=True)
            for half in range(2):
                kind, args = lastit.tiles[half - 2][2:]
                pe.wait_ge(*freed(kind, args, lastit))
                turn_tile(pe, 1, half, half)
            up(1)
            down2(0)
            pe.wait_ge(turned, GROUPS * 4)
            for half in range(2):
                out_tile(pe, 1, half, half, HEADS // 2 - 1)
            for c in range(FC):
                if c >= 1:
                    down2(c)
                if c + 2 < FC:
                    up(c + 2)
                if c == 3:
                    for late in range(EARLY, FC):
                        down_tile(pe, late, late % 2)
                if c >= 1:
                    up2(c - 1)
                if c == 2:
                    for late in range(EARLY, FC):
                        pe.wait_ge(f_out, late - EARLY + 1)
                        turn_x_tile(pe, 1, late, late % 2)
            up2(FC - 1)

        @block.vector
        def _(dve):
            def xt_part(c):
                dve.wait_ge(xt_hi, c + 1)
                cols = slice(c * 512, (c + 1) * 512)
                dve.tensor_tensor(XT[:, 1, cols], S[c % 2][:, :, :].rearrange("p a b -> p (a b)"), XT[:, 0, cols],
                                  ALU.subtract).then_inc(xt_lo, 1)

            ln_stats(dve, 0)
            ln_aggr(dve, 0)
            for c in range(PRE_CHUNKS):
                ln_apply(dve, 0, c)
            dve.wait_ge(w_in, 32)
            for w in range(2):
                src = WRAW[:, w, :].rearrange("p (h d) -> p h d", d=DH)
                for n, (kind, d0) in enumerate(((0, 0), (1, ROT))):
                    dve.wait_ge(w_hi, 2 * w + n + 1)
                    hi, lo = (WQK[:, w, hl, kind, :].rearrange("p (h d) -> p h d", d=ROT) for hl in range(2))
                    dve.scalar_tensor_tensor(lo, src[:, :, d0:d0 + ROT], WSCALE, hi, ALU.mult,
                                             ALU.subtract).then_inc(w_lo, 1)
            xt_part(0)
            xt_part(1)
            dve.wait_ge(w_hi, 5)
            dve.scalar_tensor_tensor(WV[:, 1, :], WRAW[:, 2, :], WSCALE, WV[:, 0, :], ALU.mult,
                                     ALU.subtract).then_inc(w_lo, 1)
            for n, args in enumerate(PROJ):
                dve_tile(dve, "proj", args, n + 1, 0, n % 2)
                if args[2] == "rot":
                    rot_add(dve, args, 0)
            split_out_weights(dve)
            split_ff_weights(dve)
            ln_stats(dve, 1)
            ln_aggr(dve, 1)
            for half in range(2):
                for part in range(3):
                    dve_fold(dve, half, half, part)
            dve.wait_ge(tile_made, PRE_TILES - 1)
            dve.tensor_copy(max_place(0, 0), T[0][DH:DH + 1, :]).then_inc(max_row[0], 1)

            def body(e, it):
                for k in range(SLOTS):
                    if it.first and k == 12:
                        e.wait_ge(bias_in, PRE_CHUNKS)
                    dve_slot(e, it, k)
                if it.first:
                    e.wait_ge(bias_in, FC)

            loop(dve, body)
            dve_rest(dve, END - 1, SLOTS - 1, 1)
            def rest(c):
                wait(dve, f_q, c - 1)
                for half in range(2):
                    cols = slice(half * 1024, half * 1024 + 1024)
                    dve.wait_ge(f_gelu, 4 * c + 2 * half + 2)
                    dve.tensor_tensor(HR[c % 2][:, cols], H[c % 2][:, cols],
                                      H[c % 2][:, :].bitcast(BF16)[:, half * 2048 + 1:half * 2048 + 2048:2],
                                      ALU.subtract).then_inc(f_rest, 1)

            def result(c):
                dve.wait_ge(f_bias, c + 1)
                dve.wait_ge(f_y, c + 1)
                xs = X[:, CHUNK * c:CHUNK * c + CHUNK, :]
                dve.tensor_tensor(xs, T[c % 2][:, :].rearrange("p (t d) -> p t d", d=D), xs, ALU.add).then_inc(f_out, 1)

            rest(0)
            for half in range(2):
                dve_turn(dve, half, GROUPS * 4 - 2 + half + 1, half)
            for half in range(2):
                dve.wait_ge(tile_made, tail0 + 2 + half + 1)
                xs = X[:, (B - 1) * KT + half * 4:(B - 1) * KT + half * 4 + 4, :]
                dve_add(dve, xs, half)
            dve.wait_ge(added, GROUPS * 4)
            for c in range(EARLY, FC):
                ln_stats(dve, B + c)
            for c in range(EARLY, FC):
                ln_aggr(dve, B + c)
            rest(1)
            dve.wait_ge(pv_done, 2 * END)
            for c in range(EARLY, FC):
                ln_apply(dve, 1, c)
            for c in range(2, FC):
                rest(c)
                if c == 4:
                    for late in range(EARLY, FC):
                        dve_down(dve, late, late % 2)
                result(c - 2)
                if c == 3:
                    for late in range(EARLY, FC):
                        dve_turn_x(dve, 1, late, late % 2)
            result(FC - 2)
            result(FC - 1)


def rope_table():
    inv = np.float32(1.0) / np.float32(10000.0) ** (np.arange(0, ROT, 2, dtype=np.float32) / np.float32(ROT))
    ang = np.arange(N, dtype=np.float32)[:, None] * inv[None, :]
    both = [np.tile(np.repeat(f(ang).T, 2, axis=0), (GH, 1)) for f in (np.cos, np.sin)]
    both[1][0::2] *= np.float32(-1.0)
    return np.ascontiguousarray(np.concatenate(both, axis=1).astype(np.float32))


ROPE_TABLE = rope_table()
IDENTITY = np.eye(P, dtype=np.float32)

_INS = ["L0_attn_queries", "L0_attn_Wq", "L0_attn_Wkv", "L0_attn_Wout", "L0_attn_bout", "L0_ffn_U1", "L0_ffn_V1",
        "L0_ffn_b1", "L0_ffn_U2", "L0_ffn_V2", "L0_ffn_b2"]


def kernel(**inputs):
    import concourse.bacc as bacc
    from concourse.bass_utils import run_bass_kernel_spmd

    nc = bacc.Bacc("TRN2", target_bir_lowering=False, num_devices=1)
    arrays = {f"in_{n}": np.ascontiguousarray(inputs[n]) for n in _INS}
    arrays["in_rope"], arrays["in_ident"] = ROPE_TABLE, IDENTITY
    args = [nc.dram_tensor(n, a.shape, mybir.dt.from_np(a.dtype), kind="ExternalInput").ap() for n, a in arrays.items()]
    args.append(nc.dram_tensor("out", (B, N, D), F32, kind="ExternalOutput").ap())
    build(nc, *args)
    r = run_bass_kernel_spmd(nc, [arrays], core_ids=[0])
    return r.results[0]["out"]
```
